# Optimizing a Trainium2 kernel written in Bass

```python
import numpy as np
import jax
import jax.numpy as jnp

def _softmax(x, axis=-1):
    return jax.nn.softmax(x, axis=axis)

def _gelu(x):
    return jax.nn.gelu(x, approximate=True)

def _silu(x):
    return jax.nn.silu(x)

def _sigmoid(x):
    return jax.nn.sigmoid(x)

def _layernorm(x, axis=-1, eps=1e-05):
    m = jnp.mean(x, axis=axis, keepdims=True)
    v = jnp.var(x, axis=axis, keepdims=True)
    return (x - m) / jnp.sqrt(v + eps)

def _scatter_add(tgt, idx, src, axis=0):
    return tgt.at[idx].add(src)

def _segment_sum(src, seg, n):
    return jax.ops.segment_sum(src, seg, n)
kernel_name = 'mk_adj_ffn_d1_adj_r2_43191f'

def setup_inputs(seed: int=0):
    np.random.seed(seed)
    _w = jnp.asarray

    def _rec_inputs():
        import jax
        import jax.numpy as jnp
        _gk = jax.random.key(seed)
        x = 7.22e-05 + 1 * jax.random.normal(jax.random.fold_in(_gk, 1), (2048, 256), jnp.float32)
        _a = jax.random.bernoulli(jax.random.fold_in(_gk, 2), 0.000976562, (2048, 2048))
        _a = jnp.logical_or(_a, jnp.eye(2048, dtype=bool))
        _af = _a.astype(jnp.float32)
        _af = _af * jax.random.uniform(jax.random.fold_in(_gk, 3), (2048, 2048), jnp.float32, 0.05, 1)
        adj = _af
        return (x, adj)
    x, adj = _rec_inputs()

    def _L0_gnn_setup():
        import jax, jax.numpy as jnp
        import numpy as np
        N = 8192
        F_IN = 256
        F_OUT = 256
        key = jax.random.key(seed)
        k = jax.random.split(key, 6)
        h = jax.random.normal(k[0], (N, F_IN), dtype=jnp.float32)
        adj = jax.random.uniform(k[1], (N, N), dtype=jnp.float32)
        W_neigh = jax.random.normal(k[2], (F_OUT, F_IN), dtype=jnp.float32) * (1.0 / np.sqrt(F_IN))
        b_neigh = jax.random.normal(k[3], (F_OUT,), dtype=jnp.float32) * 0.01
        W_self = jax.random.normal(k[4], (F_OUT, F_IN), dtype=jnp.float32) * (1.0 / np.sqrt(F_IN))
        b_self = jax.random.normal(k[5], (F_OUT,), dtype=jnp.float32) * 0.01
        return {'h': h, 'adj': adj, 'W_neigh': W_neigh, 'b_neigh': b_neigh, 'W_self': W_self, 'b_self': b_self}
    _L0_gnn_all = _L0_gnn_setup()
    _L0_gnn_in = {k: v for k, v in _L0_gnn_all.items() if k in ('W_neigh', 'b_neigh', 'W_self', 'b_self')}
    del _L0_gnn_all

    def _L0_ffn_setup():
        import jax, jax.numpy as jnp
        import numpy as np
        D_MODEL = 256
        N_EXPERTS = 8
        D_FF = 1024
        TOP_K = 2
        B, S = (2, 1024)
        key = jax.random.key(seed)
        ks = jax.random.split(key, 4)
        init = lambda k, shape, fan_in: jax.random.normal(k, shape, jnp.float32) / np.float32(np.sqrt(fan_in))
        return {'x': jax.random.normal(ks[0], (B, S, D_MODEL), jnp.float32), 'Wg': init(ks[1], (D_MODEL, N_EXPERTS), D_MODEL), 'bg': jnp.zeros((N_EXPERTS,), jnp.float32), 'W1': init(ks[2], (N_EXPERTS, D_MODEL, D_FF), D_MODEL), 'b1': jnp.zeros((N_EXPERTS, D_FF), jnp.float32), 'W2': init(ks[3], (N_EXPERTS, D_FF, D_MODEL), D_FF), 'b2': jnp.zeros((N_EXPERTS, D_MODEL), jnp.float32)}
    _L0_ffn_all = _L0_ffn_setup()
    _L0_ffn_in = {k: v for k, v in _L0_ffn_all.items() if k in ('Wg', 'bg', 'W1', 'b1', 'W2', 'b2')}
    del _L0_ffn_all
    return {'x': x, 'adj': adj, 'L0_gnn_W_neigh': _L0_gnn_in['W_neigh'], 'L0_gnn_b_neigh': _L0_gnn_in['b_neigh'], 'L0_gnn_W_self': _L0_gnn_in['W_self'], 'L0_gnn_b_self': _L0_gnn_in['b_self'], 'L0_ffn_Wg': _L0_ffn_in['Wg'], 'L0_ffn_bg': _L0_ffn_in['bg'], 'L0_ffn_W1': _L0_ffn_in['W1'], 'L0_ffn_b1': _L0_ffn_in['b1'], 'L0_ffn_W2': _L0_ffn_in['W2'], 'L0_ffn_b2': _L0_ffn_in['b2']}

def reference(x, adj, L0_gnn_W_neigh, L0_gnn_b_neigh, L0_gnn_W_self, L0_gnn_b_self, L0_ffn_Wg, L0_ffn_bg, L0_ffn_W1, L0_ffn_b1, L0_ffn_W2, L0_ffn_b2):
    import jax
    import jax.numpy as jnp

    def _L0_gnn_ref(h, adj, W_neigh, b_neigh, W_self, b_self):
        import jax, jax.numpy as jnp
        import numpy as np
        N = 8192
        F_IN = 256
        F_OUT = 256
        deg = jnp.sum(adj, axis=1, keepdims=True) + 1e-05
        adj_norm = adj / deg
        h_neigh = adj_norm @ h
        out = h_neigh @ W_neigh.T + b_neigh + h @ W_self.T + b_self
        return jax.nn.relu(out)

    def _L0_ffn_ref(x, Wg, bg, W1, b1, W2, b2):
        import jax, jax.numpy as jnp
        import numpy as np
        D_MODEL = 256
        N_EXPERTS = 8
        D_FF = 1024
        TOP_K = 2
        B, S = (2, 1024)
        b, s, d = x.shape
        xt = x.reshape(-1, d)
        logits = xt @ Wg + bg
        probs = jax.nn.softmax(logits, axis=-1)
        top_p, top_i = jax.lax.top_k(probs, TOP_K)
        top_p = top_p / top_p.sum(axis=-1, keepdims=True)
        T = xt.shape[0]
        combine = jnp.zeros((T, N_EXPERTS), x.dtype).at[jnp.arange(T)[:, None], top_i].add(top_p)
        h = jax.nn.relu(jnp.einsum('td,edf->etf', xt, W1) + b1[:, None, :])
        y = jnp.einsum('etf,efd->etd', h, W2) + b2[:, None, :]
        out = jnp.einsum('te,etd->td', combine, y)
        return out.reshape(b, s, d)
    x = x + _L0_gnn_ref(_layernorm(x, axis=-1), adj, L0_gnn_W_neigh, L0_gnn_b_neigh, L0_gnn_W_self, L0_gnn_b_self)
    x = x + _L0_ffn_ref(_layernorm(x, axis=-1)[None], L0_ffn_Wg, L0_ffn_bg, L0_ffn_W1, L0_ffn_b1, L0_ffn_W2, L0_ffn_b2)[0]
    return x

_drawn_inputs = setup_inputs


def setup_inputs(seed=0):
    import zlib

    import numpy as np

    out = dict(_drawn_inputs(seed))
    spreads = {'L0_ffn_bg': (0.0, 0.1), 'L0_ffn_b1': (0.0, 0.1), 'L0_ffn_b2': (0.0, 0.1)}
    factors = {'L0_gnn_b_neigh': 3.613, 'L0_gnn_b_self': 3.109}
    for name, (base, spread) in spreads.items():
        noise = np.random.default_rng([zlib.crc32(name.encode()), seed]).standard_normal(out[name].shape)
        drawn = base * np.exp(spread * noise) if base else spread * noise
        out[name] = jnp.asarray(drawn.astype(out[name].dtype))
    for name, factor in factors.items():
        out[name] = (out[name] * factor).astype(out[name].dtype)
    return out
```

```python
from contextlib import ExitStack

import concourse.bass as bass
from concourse import mybir

F32 = mybir.dt.float32
F32R = mybir.dt.float32r
BF16 = mybir.dt.bfloat16
I32 = mybir.dt.int32
U32 = mybir.dt.uint32
ALU = mybir.AluOpType
ACT = mybir.ActivationFunctionType
AX = mybir.AxisListType
Rows = bass.IndirectOffsetOnAxis

P = 128
EPS = 1e-5
TOPK = 2
SLOT = 2 * P
NOWHERE = 1 << 20


def gnn_moe_kernel(nc, x, adj_t, wn_t, ws_t, b_neigh, b_self, wg, bg, w12, b1_t, b2, out):
    N, D = x.shape
    E, F = b1_t.shape[0], b1_t.shape[1] * b1_t.shape[2]
    T = N // P
    DC = D // P
    FC = F // P
    G1 = D + 2
    HALF = N // 2
    WW = DC * F + FC * D
    WCH = WW // 4
    SLOTS = (TOPK * N + E * SLOT - 1) // SLOT
    NS = SLOTS + 1
    PAIR_ROWS = E * N + SLOT
    assert T % 2 == 0 and SLOTS % 2 == 1 and DC == 2 and FC % 2 == 0 and WCH == F

    z_rows = nc.dram_tensor("z_rows", (N, D), F32, kind="Internal").ap()
    pairs = nc.dram_tensor("pairs", (PAIR_ROWS, 4), F32, kind="Internal").ap()

    with ExitStack() as ctx:
        def sb(name, shape, dt=F32):
            return ctx.enter_context(nc.sbuf_tensor(name, shape, dt))

        def sem(name):
            return ctx.enter_context(nc.semaphore(name))

        def sems(name, n=2):
            return [sem(f"{name}{j}") for j in range(n)]

        ident = sb("ident", [P, P])
        upper = sb("upper", [P, P], BF16)
        ones = sb("ones", [P, P], BF16)
        iota_e = sb("iota_e", [P, E])
        tokens = sb("tokens", [P, T], I32)
        wg_sb = sb("wg_sb", [P, DC, E])
        bg_sb = sb("bg_sb", [P, E])
        bias_n = sb("bias_n", [P, D])
        bias_s = sb("bias_s", [P, D])
        bias = sb("bias", [P, D])
        x_sb = sb("x_sb", [P, T, D])
        self_sb = sb("self_sb", [P, T, D])
        stats = sb("stats", [P, T, 6])
        mv = sb("mv", [P, T, 2])
        ln = sb("ln", [P, 4, T])
        hn = sb("hn", [P, 2, D])
        adj_raw = sb("adj_raw", [P, 2, N])
        split = sb("split", [P, max(4 * WW, T * (G1 + D) + 4 * N)], F32R)
        zt = sb("zt", [P, 4 * D], F32R)
        x1 = sb("x1", [P, 2, D])
        xt = sb("xt", [P, D])
        z = sb("z", [P, 2, D])
        ztf = sb("ztf", [P, D])
        sm = sb("sm", [P, 16])
        lg = sb("lg", [P, E])
        top = sb("top", [P, 8])
        top_i = sb("top_i", [P, 8], U32)
        top_f = sb("top_f", [P, TOPK])
        hot = sb("hot", [P, TOPK, E])
        hot_pos = sb("hot_pos", [P, TOPK, E])
        mask = sb("mask", [P, E], BF16)
        base0 = sb("base0", [P, E])
        base = sb("base", [P, E])
        pos = sb("pos", [P, E])
        slot_f = sb("slot_f", [P, TOPK])
        slot_i = sb("slot_i", [P, 2, TOPK], I32)
        pair = sb("pair", [P, 2, TOPK, 4])
        fill = sb("fill", [P, PAIR_ROWS // P, 4])
        thr = sb("thr", [1, 8])
        tri = sb("tri", [1, E, E])
        iota_s = sb("iota_s", [1, NS])
        tb8 = sb("tb8", [1, 2, E, E])
        cnt = sb("cnt", [1, 3, E])
        ge = sb("ge", [1, 2, NS, E])
        tab_f = sb("tab_f", [1, 4, NS])
        tab = sb("tab", [1, 2, NS], I32)
        w_raw = sb("w_raw", [P, 2, WW])
        b1_sb = sb("b1_sb", [P, 2, FC])
        b2_sb = sb("b2_sb", [P, 2, D])
        slot_pair = sb("slot_pair", [P, 2, 2, 4])
        zg = sb("zg", [P, 2, 2, D])
        h_raw = sb("h_raw", [P, 2, 2 * SLOT])
        h_hi = sb("h_hi", [P, FC, SLOT], F32R)
        h_lo = sb("h_lo", [P, FC, SLOT], F32R)
        ex = sb("ex", [P, 2, 2])
        den = sb("den", [P, 2])
        coef = sb("coef", [P, 2, 2])
        y_b = sb("y_b", [P, 2 * D])
        y_c = sb("y_c", [P, 2, 2, D])

        g_hi = split[:, 0:T * G1].rearrange("p (t c) -> p t c", c=G1)
        g_lo = split[:, T * G1:T * G1 + T * D].rearrange("p (t c) -> p t c", c=D)

        def adj_split(b, part):
            at = T * (G1 + D) + (2 * b + part) * N
            return split[:, at:at + N]

        def w_split(b, part):
            return split[:, (2 * b + part) * WW:(2 * b + part + 1) * WW]

        gw_raw = y_c[:].rearrange("p b j d -> p (b j d)").rearrange("p (c f) -> p c f", c=DC)
        gw_hi = h_hi[:, 0:FC // 2, :].rearrange("p a t -> p (a t)").rearrange("p (c f) -> p c f", c=DC)
        gw_lo = h_hi[:, FC // 2:FC, :].rearrange("p a t -> p (a t)").rearrange("p (c f) -> p c f", c=DC)

        bank = [ctx.enter_context(nc.psum_tensor(f"bank{j}", [P, 512], F32)) for j in range(8)]

        x_in = sems("x_in", 4)
        gw_in, bias_in = sem("gw_in"), sem("bias_in")
        consts = sem("consts")
        fill_ready = sem("fill_ready")
        fill_out = sem("fill_out")
        dve_own = sem("dve_own")
        act_own = sem("act_own")
        var_all, std_all = sem("var_all"), sem("std_all")
        gw_split = sem("gw_split")
        hn_ready, ht_ps, ht_hi, ht_lo = sem("hn_ready"), sem("ht_ps"), sem("ht_hi"), sem("ht_lo")
        gs_ps, g_hi_ready, g_done = sem("gs_ps"), sem("g_hi_ready"), sem("g_done")
        adj_in = sems("adj_in")
        adj_hi, adj_lo = sem("adj_hi"), sem("adj_lo")
        acc_done, acc_read = sem("acc_done"), sem("acc_read")
        var_ready, std_ready, z_ready = sem("var_ready"), sem("std_ready"), sem("z_ready")
        x1_out, z_out = sems("x1_out"), sems("z_out")
        zt_r_ps, zt_r_sb, logit_ps = sem("zt_r_ps"), sem("zt_r_sb"), sem("logit_ps")
        mask_ready, rank_ps, slot_ready = sem("mask_ready"), sem("rank_ps"), sem("slot_ready")
        route = sem("route")
        place_own = sem("place_own")
        pair_out = sems("pair_out")
        table_own = sem("table_own")
        table_ready = sem("table_ready")
        w_in, b_in, pair_in = sems("w_in"), sems("b_in"), sems("pair_in")
        w_hi_ready, w_lo_ready = sem("w_hi_ready"), sem("w_lo_ready")
        z_got = [sems(f"z_got{b}_") for b in range(2)]
        zt_ps, zt_hi_ready, zt_lo_ready = sem("zt_ps"), sem("zt_hi_ready"), sem("zt_lo_ready")
        hid_ps, hid_relu, hid_hi, hid_lo = sem("hid_ps"), sem("hid_relu"), sem("hid_hi"), sem("hid_lo")
        ex_ready, coef_step = sem("ex_ready"), sem("coef_step")
        y_ps, y_biased, y_ready = sem("y_ps"), sem("y_biased"), sem("y_ready")
        y_added = sems("y_added")
        passed = {e: sem(f"passed_{e}") for e in ("sp", "pool", "dve")}

        NQ = FC // 2
        ROUTE = 13
        LN2 = 7

        def settle(eng, name):
            eng.sem_inc(passed[name], 1)

        with nc.Block() as block:

            @block.sync
            def _(sp):
                x_v = x.rearrange("(t p) d -> p t d", p=P)
                for j in range(4):
                    sp.dma_start(x_sb[:, 4 * j:4 * j + 4, :], x_v[:, 4 * j:4 * j + 4, :]).then_inc(x_in[j], 16)
                sp.dma_start(gw_raw[:, :, 0:D], wn_t.rearrange("(c p) f -> p c f", p=P)).then_inc(gw_in, 16)
                sp.dma_start(gw_raw[:, :, D:2 * D], ws_t.rearrange("(c p) f -> p c f", p=P)).then_inc(gw_in, 16)
                sp.dma_start(bias_n[:], b_neigh[None, :].to_broadcast([P, D])).then_inc(bias_in, 16)
                sp.dma_start(bias_s[:], b_self[None, :].to_broadcast([P, D])).then_inc(bias_in, 16)
                sp.dma_start(wg_sb[:], wg.rearrange("(c p) e -> p c e", p=P)).then_inc(bias_in, 16)
                sp.dma_start(bg_sb[:], bg[None, :].to_broadcast([P, E])).then_inc(bias_in, 16)
                for b in range(2):
                    sp.dma_start(adj_raw[:, b, :], adj_t[b]).then_inc(adj_in[b], 16)
                sp.wait_ge(fill_ready, 2)
                sp.dma_start(pairs.rearrange("(p r) w -> p r w", p=P), fill[:]).then_inc(fill_out, 16)
                sp.dma_start(w_raw[:, 0, :], w12[0]).then_inc(w_in[0], 16)
                sp.dma_start(b1_sb[:, 0, :], b1_t[0]).then_inc(b_in[0], 16)
                sp.dma_start(b2_sb[:, 0, :], b2[0:1, :].to_broadcast([P, D])).then_inc(b_in[0], 16)
                for b in range(2):
                    sp.wait_ge(adj_lo, 2 * b + 2)
                    sp.dma_start(adj_raw[:, b, :], adj_t[2 + b]).then_inc(adj_in[b], 16)

                def store(i, b):
                    sp.wait_ge(z_ready, i + 1)
                    sp.dma_start(out[bass.ds(i * P, P), :], x1[:, b, :]).then_inc(x1_out[b], 16)
                    sp.dma_start(z_rows[bass.ds(i * P, P), :], z[:, b, :]).then_inc(z_out[b], 16)

                with sp.Fori(0, T // 2 - 2) as k:
                    for b in range(2):
                        store(2 * k + b, b)
                        sp.wait_ge(adj_lo, 4 * k + 2 * b + 6)
                        sp.dma_start(adj_raw[:, b, :], adj_t[bass.ds(2 * k + b + 4, 1)].rearrange("a p n -> (a p) n")).then_inc(adj_in[b], 16)
                for i in range(T - 4, T):
                    store(i, i % 2)

                for c in range(TOPK):
                    sp.wait_ge(pair_out[c], 16 * T)
                sp.wait_ge(table_ready, 1)

                def load_slot(s, b, weights=True):
                    if not isinstance(s, int) or s >= 2:
                        sp.wait_ge(w_lo_ready, 4 * s - 4)
                        settle(sp, "sp")
                        sp.wait_ge(y_biased, s - 1)
                        settle(sp, "sp")
                        sp.wait_ge(y_added[0], 16 * s - 16)
                        sp.wait_ge(y_added[1], 16 * s - 16)
                        settle(sp, "sp")
                    at = sp.value_load(tab[0:1, 1, bass.ds(s, 1)], min_val=0, max_val=E * N)
                    rows = pairs[bass.ds(at, SLOT), :].rearrange("(j p) w -> p j w", p=P)
                    sp.dma_start(slot_pair[:, b, :, :], rows).then_inc(pair_in[b], 16)
                    if weights:
                        e = sp.value_load(tab[0:1, 0, bass.ds(s, 1)], min_val=0, max_val=E - 1)
                        sp.dma_start(w_raw[:, b, :], w12[bass.ds(e, 1)].rearrange("a p n -> (a p) n")).then_inc(w_in[b], 16)
                        sp.dma_start(b1_sb[:, b, :], b1_t[bass.ds(e, 1)].rearrange("a p n -> (a p) n")).then_inc(b_in[b], 16)
                        sp.dma_start(b2_sb[:, b, :], b2[bass.ds(e, 1), :].to_broadcast([P, D])).then_inc(b_in[b], 16)

                load_slot(0, 0, weights=False)
                load_slot(1, 1)
                with sp.Fori(1, SLOTS // 2) as k:
                    for b in range(2):
                        load_slot(2 * k + b, b)
                load_slot(SLOTS - 1, 0)
                for j in range(2):
                    sp.wait_ge(y_added[j], 16 * SLOTS)
                    sp.wait_ge(x1_out[j], 16 * T // 2)

            @block.gpsimd
            def _(pool):
                pool.memset(ident[:], 0.0).then_inc(fill_ready, 1)
                pool.memset(upper[:], 1.0)
                pool.memset(ones[:], 1.0)
                pool.memset(fill[:], 0.0)
                pool.memset(pair[:], 0.0)
                pool.memset(zg[:], 0.0)
                pool.memset(tri[:], 1.0)
                pool.memset(g_hi[:, :, D:D + 1].bitcast(F32), 1.0)
                pool.memset(g_hi[:, :, D + 1:D + 2].bitcast(F32), 0.0)
                pool.iota(thr[:], [[SLOT, 8]], base=0, channel_multiplier=0, allow_small_or_imprecise_dtypes=True)
                pool.iota(iota_s[:], [[1, NS]], base=0, channel_multiplier=0, allow_small_or_imprecise_dtypes=True)
                pool.iota(iota_e[:], [[1, E]], base=0, channel_multiplier=0, allow_small_or_imprecise_dtypes=True)
                pool.iota(base0[:], [[N, E]], base=0, channel_multiplier=0, allow_small_or_imprecise_dtypes=True)
                pool.iota(base[:], [[N, E]], base=0, channel_multiplier=0, allow_small_or_imprecise_dtypes=True)
                pool.iota(tokens[:], [[P, T]], base=0, channel_multiplier=1).then_inc(consts, 1)
                pool.wait_ge(consts, 1)
                pool.memset(fill[:, :, 0:1].bitcast(I32), NOWHERE).then_inc(fill_ready, 1)
                pool.affine_select(ident[:], ident[:], [[-1, P]], ALU.not_equal, 1.0, base=0, channel_multiplier=1)
                pool.affine_select(upper[:], upper[:], [[1, P]], ALU.is_gt, 0.0, base=0, channel_multiplier=-1)
                pool.affine_select(tri[:], tri[:], [[1, E], [-1, E]], ALU.is_ge, 0.0, base=0, channel_multiplier=0)
                pool.memset(thr[:, 0:1], -1.0).then_inc(consts, 1)

                pool.wait_ge(fill_out, 16)

                def scatter(i, b):
                    pool.wait_ge(slot_ready, i + 1)
                    settle(pool, "pool")
                    for c in range(TOPK):
                        pool.indirect_dma_start(pairs, Rows(slot_i[:, b, c:c + 1], 0), pair[:, b, c, :],
                                                None).then_inc(pair_out[c], 16)
                    for c in range(TOPK):
                        pool.wait_ge(pair_out[c], 16 * i + 16)
                    settle(pool, "pool")

                with pool.Fori(0, T // 2) as k:
                    for b in range(2):
                        scatter(2 * k + b, b)

                for b in range(2):
                    pool.wait_ge(z_out[b], 16 * T // 2)
                    pool.wait_ge(x1_out[b], 16 * T // 2)

                def gather(s, b, k):
                    pool.wait_ge(pair_in[b], 16 * k + 16)
                    if not isinstance(s, int) or s >= 2:
                        pool.wait_ge(zt_ps, s - 1)
                    settle(pool, "pool")
                    for j in range(2):
                        pool.indirect_dma_start(zg[:, b, j, :], None, z_rows, Rows(slot_pair[:, b, j, 0:1].bitcast(I32), 0),
                                                bounds_check=N - 1, oob_is_err=False).then_inc(z_got[b][j], 16)

                def add(s, b):
                    pool.wait_ge(y_ready, 2 * s + 2)
                    settle(pool, "pool")
                    for j in range(2):
                        pool.indirect_dma_start(out, Rows(slot_pair[:, b, j, 0:1].bitcast(I32), 0), y_c[:, b, j, :], None,
                                                bounds_check=N - 1, oob_is_err=False,
                                                compute_op=ALU.add).then_inc(y_added[j], 16)
                    for j in range(2):
                        pool.wait_ge(y_added[j], 16 * s + 16)
                    settle(pool, "pool")

                gather(0, 0, 0)
                gather(1, 1, 0)
                with pool.Fori(0, SLOTS // 2 - 1) as k:
                    for b in range(2):
                        add(2 * k + b, b)
                        gather(2 * k + b + 2, b, k + 1)
                add(SLOTS - 3, 0)
                gather(SLOTS - 1, 0, SLOTS // 2)
                add(SLOTS - 2, 1)
                add(SLOTS - 1, 0)

            @block.scalar
            def _(act):
                act.wait_ge(gw_in, 32)
                act.activation(gw_hi[:], gw_raw[:], ACT.Copy).then_inc(gw_split, 1)
                act.wait_ge(var_all, 1)
                act.activation(ln[:, 1, :], ln[:, 0, :], ACT.Sqrt).then_inc(std_all, 1)

                def features(i, b):
                    act.wait_ge(ht_ps, i + 1)
                    act.activation(zt[:, 2 * D * b:2 * D * b + D], bank[b][:, 0:D], ACT.Copy).then_inc(ht_hi, 1)
                    act.wait_ge(gs_ps, i + 1)
                    act.activation(g_hi[:, bass.ds(i, 1), 0:D], bank[2 + b][:, None, 0:D], ACT.Copy).then_inc(g_hi_ready, 1)

                with act.Fori(0, T // 2) as k:
                    for b in range(2):
                        features(2 * k + b, b)

                def high(i, b, half, k):
                    act.wait_ge(adj_in[b], 16 * k + 16)
                    cols = slice(half * HALF, half * HALF + HALF)
                    act.activation(adj_split(b, 0)[:, cols], adj_raw[:, b, cols], ACT.Copy).then_inc(adj_hi, 1)

                def root(i):
                    act.wait_ge(var_ready, i + 1)
                    act.activation(sm[:, 4:5], sm[:, 3:4], ACT.Sqrt).then_inc(std_ready, 1)

                def logits_in(i):
                    act.wait_ge(zt_r_ps, i + 1)
                    act.activation(ztf[:], bank[6][:, 0:D], ACT.Copy).then_inc(zt_r_sb, 1)

                for b in range(2):
                    for half in range(2):
                        high(b, b, half, 0)
                with act.Fori(0, T // 2 - 1) as k:
                    for b in range(2):
                        i = 2 * k + b
                        act.wait_ge(acc_done, i + 1)
                        high(i + 2, b, 0, k + 1)
                        root(i)
                        high(i + 2, b, 1, k + 1)
                        logits_in(i)
                for i in (T - 2, T - 1):
                    root(i)
                    logits_in(i)

                def high_w(b, c, k):
                    act.wait_ge(w_in[b], 16 * k + 16)
                    cols = slice(c * WCH, c * WCH + WCH)
                    act.activation(w_split(b, 0)[:, cols], w_raw[:, b, cols], ACT.Copy).then_inc(w_hi_ready, 1)

                def high_z(s):
                    act.wait_ge(zt_ps, s + 1)
                    act.activation(zt[:, 0:2 * D], bank[6][:], ACT.Copy).then_inc(zt_hi_ready, 1)

                def slot(s, b, k, more=True):
                    act.wait_ge(pair_in[b], 16 * k + 16)
                    if not isinstance(s, int) or s >= 1:
                        act.wait_ge(coef_step, 3 * s)
                    act.activation(ex[:], slot_pair[:, b, :, 1:3], ACT.Exp).then_inc(ex_ready, 1)
                    act.wait_ge(b_in[b], 32 * k + 32)
                    if more:
                        act.wait_ge(y_ps, s)
                    for q in range(NQ):
                        act.wait_ge(hid_ps, NQ * s + q + 1)
                        if not isinstance(s, int) or s > 0 or q >= 2:
                            act.wait_ge(hid_lo, NQ * s + q - 1)
                        for c in range(2):
                            act.activation(h_raw[:, q % 2, c * SLOT:c * SLOT + SLOT], bank[2 + q][:, c * SLOT:c * SLOT + SLOT],
                                           ACT.Relu, bias=b1_sb[:, b, 2 * q + c:2 * q + c + 1]).then_inc(hid_relu, 1)
                        if more:
                            high_w(1 - b, q, k + b)
                    if more:
                        high_z(s + 1)
                    act.wait_ge(y_biased, s + 1)
                    act.wait_ge(coef_step, 3 * s + 3)
                    if not isinstance(s, int) or s >= 2:
                        act.wait_ge(y_added[0], 16 * s - 16)
                        act.wait_ge(y_added[1], 16 * s - 16)
                    for j in range(2):
                        act.activation(y_c[:, b, j, :], y_b[:, j * D:j * D + D], ACT.Copy,
                                       scale=coef[:, b, j:j + 1]).then_inc(y_ready, 1)

                act.wait_ge(acc_done, T)
                for c in range(4):
                    high_w(0, c, 0)
                high_z(0)
                for s in range(2):
                    slot(s, s, 0)
                with act.Fori(1, SLOTS // 2) as k:
                    for b in range(2):
                        slot(2 * k + b, b, k)
                slot(SLOTS - 1, 0, SLOTS // 2, more=False)

            @block.vector
            def _(dve):
                own = [0]

                def link(ins):
                    own[0] += 1
                    ins.then_inc(dve_own, 1)
                    dve.wait_ge(dve_own, own[0])

                for j in range(4):
                    dve.wait_ge(x_in[j], 16)
                    for t in range(4 * j, 4 * j + 4):
                        last = dve.bn_stats(stats[:, t, :], x_sb[:, t, :])
                link(last)
                for t in range(T):
                    last = dve.bn_aggr(mv[:, t, :], stats[:, t, :])
                link(last)
                dve.tensor_scalar(ln[:, 0, :], mv[:, :, 1], EPS, None, ALU.add).then_inc(var_all, 1)
                dve.wait_ge(bias_in, 64)
                dve.tensor_tensor(bias[:], bias_n[:], bias_s[:], ALU.add)
                dve.wait_ge(gw_split, 1)
                dve.tensor_tensor(gw_lo[:], gw_raw[:], gw_hi[:], ALU.subtract).then_inc(gw_split, 1)
                dve.wait_ge(std_all, 1)
                link(dve.reciprocal(ln[:, 1, :], ln[:, 1, :]))
                link(dve.tensor_tensor(ln[:, 2, :], ln[:, 0, :], ln[:, 1, :], ALU.mult))
                link(dve.tensor_tensor(ln[:, 2, :], ln[:, 2, :], ln[:, 1, :], ALU.mult))
                link(dve.tensor_scalar(ln[:, 2, :], ln[:, 2, :], -0.5, 1.5, ALU.mult, ALU.add))
                link(dve.tensor_tensor(ln[:, 3, :], ln[:, 1, :], ln[:, 2, :], ALU.mult))

                def normed(i, b):
                    dve.tensor_scalar(hn[:, b, None, :], x_sb[:, bass.ds(i, 1), :], mv[:, bass.ds(i, 1), 0], ln[:, 3, bass.ds(i, 1)],
                                      ALU.subtract, ALU.mult).then_inc(hn_ready, 1)

                normed(0, 0)
                normed(1, 1)

                def features(i, b, more=True):
                    dve.wait_ge(ht_hi, i + 1)
                    dve.tensor_tensor(zt[:, 2 * D * b + D:2 * D * b + 2 * D], bank[b][:, 0:D], zt[:, 2 * D * b:2 * D * b + D],
                                      ALU.subtract).then_inc(ht_lo, 1)
                    if more:
                        normed(i + 2, b)
                    dve.wait_ge(g_hi_ready, i + 1)
                    dve.tensor_tensor(g_lo[:, bass.ds(i, 1), :], bank[2 + b][:, None, 0:D], g_hi[:, bass.ds(i, 1), 0:D],
                                      ALU.subtract)
                    dve.tensor_tensor(self_sb[:, bass.ds(i, 1), :], bank[2 + b][:, None, D:2 * D], bias[:, None, :],
                                      ALU.add).then_inc(g_done, 1)

                with dve.Fori(0, T // 2 - 1) as k:
                    for b in range(2):
                        features(2 * k + b, b)
                for i in (T - 2, T - 1):
                    features(i, i % 2, more=False)

                def low(i, b, half, k):
                    dve.wait_ge(adj_hi, 2 * i + half + 1)
                    cols = slice(half * HALF, half * HALF + HALF)
                    dve.tensor_tensor(adj_split(b, 1)[:, cols], adj_raw[:, b, cols], adj_split(b, 0)[:, cols],
                                      ALU.subtract).then_inc(adj_lo, 1)

                first = own[0]
                for b in range(2):
                    for half in range(2):
                        low(b, b, half, 0)
                dve.wait_ge(g_done, T)
                dve.wait_ge(consts, 2)

                def residual(i, b, k):
                    n = [0]

                    def step(ins, plain=False):
                        n[0] += 1
                        ins.then_inc(dve_own, 1)
                        dve.wait_ge(dve_own, LN2 * i + first + n[0])
                        if plain:
                            settle(dve, "dve")

                    dve.wait_ge(acc_done, i + 1)
                    step(dve.tensor_scalar(sm[:, 0:1], bank[b][:, D:D + 1], EPS, None, ALU.add))
                    step(dve.reciprocal(sm[:, 1:2], sm[:, 0:1]))
                    dve.scalar_tensor_tensor(out=xt[:, None, :], in0=bank[b][:, None, 0:D], scalar=sm[:, 1:2], in1=self_sb[:, bass.ds(i, 1), :],
                                             op0=ALU.mult, op1=ALU.add).then_inc(acc_read, 1)
                    dve.wait_ge(acc_read, i + 1)
                    dve.wait_ge(x1_out[b], 16 * k)
                    dve.wait_ge(z_out[b], 16 * k)
                    step(dve.scalar_tensor_tensor(out=x1[:, b, None, :], in0=xt[:, None, :], scalar=0.0, in1=x_sb[:, bass.ds(i, 1), :],
                                                  op0=ALU.max, op1=ALU.add))
                    step(dve.bn_stats(stats[:, 0, :], x1[:, b, :]), plain=True)
                    step(dve.bn_aggr(mv[:, 0, :], stats[:, 0, :]))
                    dve.tensor_scalar(sm[:, 3:4], mv[:, 0, 1:2], EPS, None, ALU.add).then_inc(var_ready, 1)
                    dve.wait_ge(std_ready, i + 1)
                    step(dve.reciprocal(sm[:, 5:6], sm[:, 4:5]))
                    step(dve.scalar_tensor_tensor(out=sm[:, 6:7], in0=sm[:, 5:6], scalar=sm[:, 3:4], in1=sm[:, 5:6],
                                                  op0=ALU.mult, op1=ALU.mult))
                    assert n[0] == LN2

                def residual_end(i, b):
                    link2 = ROUTE * i
                    dve.tensor_scalar(sm[:, 7:8], sm[:, 6:7], -0.5, 1.5, ALU.mult, ALU.add).then_inc(route, 1)
                    dve.wait_ge(route, link2 + 1)
                    dve.tensor_tensor(sm[:, 8:9], sm[:, 5:6], sm[:, 7:8], ALU.mult).then_inc(route, 1)
                    dve.wait_ge(route, link2 + 2)
                    dve.tensor_scalar(z[:, b, :], x1[:, b, :], mv[:, 0, 0:1], sm[:, 8:9], ALU.subtract,
                                      ALU.mult).then_inc(z_ready, 1)

                def choose(i, b, k):
                    n = [2]

                    def step(ins, wait=True, plain=False):
                        n[0] += 1
                        ins.then_inc(route, 1)
                        if wait:
                            dve.wait_ge(route, ROUTE * i + n[0])
                        if plain:
                            settle(dve, "dve")

                    dve.wait_ge(logit_ps, i + 1)
                    step(dve.tensor_tensor(lg[:], bank[7][:, 0:E], bg_sb[:], ALU.add), plain=True)
                    step(dve.max(top[:], lg[:]), plain=True)
                    step(dve.max_index(top_i[:], top[:], lg[:]))
                    step(dve.tensor_copy(top_f[:], top_i[:, 0:TOPK]))
                    for c in range(TOPK):
                        step(dve.tensor_scalar(hot[:, c, :], iota_e[:], top_f[:, c:c + 1], None, ALU.is_equal), wait=c > 0)
                    dve.tensor_tensor(mask[:], hot[:, 0, :], hot[:, 1, :], ALU.add).then_inc(mask_ready, 1)
                    for c in range(TOPK):
                        dve.wait_ge(pair_out[c], 16 * i if k is None else 16 * i)
                    for c in range(TOPK):
                        dve.tensor_copy(pair[:, b, c, None, 0:1].bitcast(I32), tokens[:, None, bass.ds(i, 1)])
                        step(dve.tensor_tensor(pair[:, b, c, 1:2], top[:, 1:2], top[:, 0:1], ALU.subtract), wait=False)
                    step(dve.tensor_tensor(pair[:, b, 1, 2:3], top[:, 1:2], top[:, 0:1], ALU.subtract), wait=False)

                def place(i, b):
                    def step(ins, n):
                        ins.then_inc(route, 1)
                        dve.wait_ge(route, ROUTE * i + n)

                    dve.wait_ge(rank_ps, i + 1)
                    step(dve.tensor_tensor(pos[:], bank[5][:, 0:E], base[:], ALU.add), 12)
                    dve.tensor_tensor(base[:], bank[5][:, E:2 * E], base[:], ALU.add)
                    for c in range(TOPK):
                        last = dve.tensor_tensor(hot_pos[:, c, :], hot[:, c, :], pos[:], ALU.mult)
                    step(last, 13)
                    dve.tensor_reduce(slot_f[:], hot_pos[:], AX.X, ALU.add).then_inc(place_own, 1)
                    dve.wait_ge(place_own, i + 1)
                    dve.tensor_copy(slot_i[:, b, :], slot_f[:]).then_inc(slot_ready, 1)

                with dve.Fori(0, T // 2 - 1) as k:
                    for b in range(2):
                        i = 2 * k + b
                        residual(i, b, k)
                        residual_end(i, b)
                        low(i + 2, b, 0, k + 1)
                        choose(i, b, k)
                        low(i + 2, b, 1, k + 1)
                        place(i, b)
                for i in (T - 2, T - 1):
                    residual(i, i % 2, T // 2 - 1)
                    residual_end(i, i % 2)
                    choose(i, i % 2, T // 2 - 1)
                    place(i, i % 2)

                tn = [0]

                def tlink(ins):
                    tn[0] += 1
                    ins.then_inc(table_own, 1)
                    dve.wait_ge(table_own, tn[0])

                r0 = slice(0, 1)
                dve.wait_ge(slot_ready, T)
                tlink(dve.tensor_tensor(cnt[:, 0, :], base[r0, :], base0[r0, :], ALU.subtract))
                tlink(dve.tensor_tensor(tb8[:, 0], cnt[:, 0, :, None].to_broadcast([1, E, E]), thr[:, None, :].to_broadcast([1, E, 8]), ALU.is_gt))
                tlink(dve.tensor_reduce(cnt[:, 1, :], tb8[:, 0], AX.X, ALU.add))
                tlink(dve.tensor_tensor(tb8[:, 1], tri[:], cnt[:, 1, None, :].to_broadcast([1, E, E]), ALU.mult))
                tlink(dve.tensor_reduce(cnt[:, 2, :], tb8[:, 1], AX.X, ALU.add))
                tlink(dve.tensor_tensor(ge[:, 0], iota_s[:, :, None].to_broadcast([1, NS, E]), cnt[:, 2, None, :].to_broadcast([1, NS, E]), ALU.is_ge))
                dve.tensor_reduce(tab_f[:, 0, :], ge[:, 0], AX.X, ALU.add)
                tlink(dve.tensor_tensor(ge[:, 1], ge[:, 0], cnt[:, 1, None, :].to_broadcast([1, NS, E]), ALU.mult))
                tlink(dve.tensor_reduce(tab_f[:, 1, :], ge[:, 1], AX.X, ALU.add))
                tlink(dve.tensor_tensor(tab_f[:, 2, :], iota_s[:], tab_f[:, 1, :], ALU.subtract))
                tlink(dve.tensor_scalar(tab_f[:, 2, :], tab_f[:, 2, :], float(SLOT), None, ALU.mult))
                tlink(dve.scalar_tensor_tensor(out=tab_f[:, 3, :], in0=tab_f[:, 0, :], scalar=float(N), in1=tab_f[:, 2, :],
                                               op0=ALU.mult, op1=ALU.add))
                dve.tensor_scalar(tab[:, 0, :], tab_f[:, 0, :], float(E - 1), None, ALU.min)
                dve.tensor_scalar(tab[:, 1, :], tab_f[:, 3, :], float(E * N), None, ALU.min).then_inc(table_ready, 1)

                def low_w(b, c, s):
                    dve.wait_ge(w_hi_ready, 4 * s + c + 1)
                    cols = slice(c * WCH, c * WCH + WCH)
                    dve.tensor_tensor(w_split(b, 1)[:, cols], w_raw[:, b, cols], w_split(b, 0)[:, cols],
                                      ALU.subtract).then_inc(w_lo_ready, 1)

                def low_z(s):
                    dve.wait_ge(zt_hi_ready, s + 1)
                    dve.tensor_tensor(zt[:, 2 * D:4 * D], bank[6][:], zt[:, 0:2 * D], ALU.subtract).then_inc(zt_lo_ready, 1)

                def slot(s, b, k, more=True):
                    dve.wait_ge(ex_ready, s + 1)
                    if not isinstance(s, int) or s >= 2:
                        dve.wait_ge(y_ready, 2 * s - 2)
                    dve.tensor_scalar(den[:], ex[:, :, 0], 1.0, None, ALU.add).then_inc(coef_step, 1)
                    dve.wait_ge(coef_step, 3 * s + 1)
                    dve.reciprocal(den[:], den[:]).then_inc(coef_step, 1)
                    dve.wait_ge(coef_step, 3 * s + 2)
                    dve.tensor_tensor(coef[:, b, :], den[:], ex[:, :, 1], ALU.mult).then_inc(coef_step, 1)
                    for q in range(NQ):
                        dve.wait_ge(hid_relu, 2 * NQ * s + 2 * q + 2)
                        dve.tensor_copy(h_hi[:, 2 * q:2 * q + 2, :].rearrange("p a t -> p (a t)"), h_raw[:, q % 2, :]).then_inc(hid_hi, 1)
                        dve.wait_ge(hid_hi, NQ * s + q + 1)
                        dve.tensor_tensor(h_lo[:, 2 * q:2 * q + 2, :].rearrange("p a t -> p (a t)"), h_raw[:, q % 2, :],
                                          h_hi[:, 2 * q:2 * q + 2, :].rearrange("p a t -> p (a t)"),
                                          ALU.subtract).then_inc(hid_lo, 1)
                        if more:
                            low_w(1 - b, q, s + 1)
                    if more:
                        low_z(s + 1)
                    dve.wait_ge(y_ps, s + 1)
                    if not isinstance(s, int) or s >= 1:
                        dve.wait_ge(y_ready, 2 * s)
                    dve.tensor_tensor(y_b[:].rearrange("p (j d) -> p j d", j=2), bank[b][:].rearrange("p (j d) -> p j d", j=2),
                                      b2_sb[:, b, None, :].to_broadcast([P, 2, D]), ALU.add).then_inc(y_biased, 1)

                for c in range(4):
                    low_w(0, c, 0)
                low_z(0)
                for s in range(2):
                    slot(s, s, 0)
                with dve.Fori(1, SLOTS // 2) as k:
                    for b in range(2):
                        slot(2 * k + b, b, k)
                slot(SLOTS - 1, 0, SLOTS // 2, more=False)

            @block.tensor
            def _(pe):
                pe.wait_ge(consts, 2)

                def rows_t(i, b):
                    pe.wait_ge(hn_ready, i + 1)
                    if not isinstance(i, int) or i >= 2:
                        pe.wait_ge(ht_lo, i - 1)
                    for c in range(DC):
                        last = pe.transpose(bank[b][:, c * P:c * P + P], hn[:, b, c * P:c * P + P], ident[:])
                    last.then_inc(ht_ps, 1)

                def products(out_ap, terms):
                    for n, (o, w, m) in enumerate(terms):
                        last = pe.matmul(o, w, m, start=(n == 0), stop=(n == len(terms) - 1), skip_group_check=True)
                    return last

                def features(i, b):
                    pe.wait_ge(ht_lo, i + 1)
                    if not isinstance(i, int) or i >= 2:
                        pe.wait_ge(g_done, i - 1)
                    hi, lo = zt[:, 2 * D * b:2 * D * b + D], zt[:, 2 * D * b + D:2 * D * b + 2 * D]
                    terms = []
                    for c in range(DC):
                        cc = slice(c * P, c * P + P)
                        terms += [(bank[2 + b][:], hi[:, cc], gw_hi[:, c, :]), (bank[2 + b][:], hi[:, cc], gw_lo[:, c, :]),
                                  (bank[2 + b][:], lo[:, cc], gw_hi[:, c, :])]
                    products(None, terms).then_inc(gs_ps, 1)

                pe.wait_ge(gw_split, 2)
                rows_t(0, 0)
                rows_t(1, 1)
                for i in range(2):
                    features(i, i)
                    rows_t(i + 2, i)
                with pe.Fori(1, T // 2 - 1) as k:
                    for b in range(2):
                        features(2 * k + b, b)
                        rows_t(2 * k + b + 2, b)
                for i in (T - 2, T - 1):
                    features(i, i % 2)

                def aggregate(b, j0, j1):
                    hi, lo = adj_split(b, 0), adj_split(b, 1)
                    for j in range(j0, j1):
                        jj = slice(j * P, j * P + P)
                        pe.matmul(bank[b][:, 0:G1], hi[:, jj], g_hi[:, j, :], start=(j == 0), stop=False, skip_group_check=True)
                        pe.matmul(bank[b][:, 0:D], hi[:, jj], g_lo[:, j, :], start=False, stop=False, skip_group_check=True)
                        last = pe.matmul(bank[b][:, 0:G1], lo[:, jj], g_hi[:, j, :], start=False, stop=(j == T - 1),
                                         skip_group_check=True)
                    return last

                def transpose_z(i, b):
                    pe.wait_ge(z_ready, i + 1)
                    if not isinstance(i, int) or i >= 1:
                        pe.wait_ge(zt_r_sb, i)
                    for c in range(DC):
                        last = pe.transpose(bank[6][:, c * P:c * P + P], z[:, b, c * P:c * P + P], ident[:])
                    last.then_inc(zt_r_ps, 1)

                def logits(i):
                    pe.wait_ge(zt_r_sb, i + 1)
                    if not isinstance(i, int) or i >= 1:
                        pe.wait_ge(mask_ready, i)
                    for c in range(DC):
                        last = pe.matmul(bank[7][:, 0:E], ztf[:, c * P:c * P + P], wg_sb[:, c, :], start=(c == 0), stop=(c == DC - 1))
                    last.then_inc(logit_ps, 1)

                def ranks(i):
                    pe.wait_ge(mask_ready, i + 1)
                    if not isinstance(i, int) or i >= 1:
                        pe.wait_ge(slot_ready, i)
                    pe.matmul(bank[5][:, 0:E], upper[:], mask[:], start=True, stop=True)
                    pe.matmul(bank[5][:, E:2 * E], ones[:], mask[:], start=True, stop=True).then_inc(rank_ps, 1)

                def tile(i, b, route_last=True):
                    pe.wait_ge(adj_lo, 2 * i + 1)
                    if route_last:
                        pe.wait_ge(acc_read, i - 1)
                    aggregate(b, 0, T // 2)
                    if route_last:
                        transpose_z(i - 1, 1 - b)
                    pe.wait_ge(adj_lo, 2 * i + 2)
                    aggregate(b, T // 2, 3 * T // 4)
                    if route_last:
                        logits(i - 1)
                    aggregate(b, 3 * T // 4, T).then_inc(acc_done, 1)
                    if route_last:
                        ranks(i - 1)

                pe.wait_ge(g_done, T)
                tile(0, 0, route_last=False)
                tile(1, 1)
                with pe.Fori(1, T // 2) as k:
                    for b in range(2):
                        tile(2 * k + b, b)
                transpose_z(T - 1, 1)
                logits(T - 1)
                ranks(T - 1)

                def transpose_slot(s, b, k):
                    for j in range(2):
                        pe.wait_ge(z_got[b][j], 16 * k + 16)
                    if not isinstance(s, int) or s >= 1:
                        pe.wait_ge(zt_lo_ready, s)
                    for j in range(2):
                        for c in range(DC):
                            last = pe.transpose(bank[6][:, c * SLOT + j * P:c * SLOT + j * P + P], zg[:, b, j, c * P:c * P + P], ident[:])
                    last.then_inc(zt_ps, 1)

                def slot(s, b, k, more=True):
                    w_hi, w_lo = w_split(b, 0), w_split(b, 1)
                    z_hi, z_lo = zt[:, 0:2 * D], zt[:, 2 * D:4 * D]
                    pe.wait_ge(zt_lo_ready, s + 1)
                    pe.wait_ge(w_lo_ready, 4 * s + 2)
                    for q in range(NQ):
                        if not isinstance(s, int) or s >= 1:
                            pe.wait_ge(hid_relu, 2 * NQ * s - 2 * NQ + 2 * q + 2)
                        for c in range(2):
                            o = bank[2 + q][:, c * SLOT:c * SLOT + SLOT]
                            terms = []
                            for d in range(DC):
                                f = slice(d * F + (2 * q + c) * P, d * F + (2 * q + c) * P + P)
                                t = slice(d * SLOT, d * SLOT + SLOT)
                                terms += [(o, w_hi[:, f], z_hi[:, t]), (o, w_hi[:, f], z_lo[:, t]), (o, w_lo[:, f], z_hi[:, t])]
                            last = products(o, terms)
                        last.then_inc(hid_ps, 1)
                    if more:
                        transpose_slot(s + 1, 1 - b, k + b)
                    pe.wait_ge(w_lo_ready, 4 * s + 4)
                    if not isinstance(s, int) or s >= 2:
                        pe.wait_ge(y_biased, s - 1)
                    for j in range(2):
                        o = bank[b][:, j * D:j * D + D]
                        t = slice(j * P, j * P + P)
                        for c in range(FC):
                            if j == 0 and c % 2 == 0:
                                pe.wait_ge(hid_lo, NQ * s + c // 2 + 1)
                            d = slice(DC * F + c * D, DC * F + c * D + D)
                            pe.matmul(o, h_hi[:, c, t], w_hi[:, d], start=(c == 0), stop=False, skip_group_check=True)
                            pe.matmul(o, h_hi[:, c, t], w_lo[:, d], start=False, stop=False, skip_group_check=True)
                            last = pe.matmul(o, h_lo[:, c, t], w_hi[:, d], start=False, stop=(c == FC - 1), skip_group_check=True)
                    last.then_inc(y_ps, 1)

                transpose_slot(0, 0, 0)
                for s in range(2):
                    slot(s, s, 0)
                with pe.Fori(1, SLOTS // 2) as k:
                    for b in range(2):
                        slot(2 * k + b, b, k)
                slot(SLOTS - 1, 0, SLOTS // 2, more=False)


def kernel(x, adj, L0_gnn_W_neigh, L0_gnn_b_neigh, L0_gnn_W_self, L0_gnn_b_self, L0_ffn_Wg, L0_ffn_bg,
           L0_ffn_W1, L0_ffn_b1, L0_ffn_W2, L0_ffn_b2):
    import numpy as np
    import concourse.bacc as bacc
    from concourse.bass_utils import run_bass_kernel_spmd

    x, adj, w1, b1, w2, b2 = (np.asarray(a) for a in (x, adj, L0_ffn_W1, L0_ffn_b1, L0_ffn_W2, L0_ffn_b2))
    n, (e, d, f) = x.shape[0], w1.shape
    t, dc, fc = n // P, d // P, f // P
    arrays = {
        "x": x,
        "adj_t": adj.reshape(t, P, t, P).transpose(0, 3, 2, 1).reshape(t, P, n),
        "wn_t": np.asarray(L0_gnn_W_neigh).T,
        "ws_t": np.asarray(L0_gnn_W_self).T,
        "b_neigh": np.asarray(L0_gnn_b_neigh),
        "b_self": np.asarray(L0_gnn_b_self),
        "wg": np.asarray(L0_ffn_Wg),
        "bg": np.asarray(L0_ffn_bg),
        "w12": np.concatenate([w1.reshape(e, dc, P, f).transpose(0, 2, 1, 3).reshape(e, P, dc * f),
                               w2.reshape(e, fc, P, d).transpose(0, 2, 1, 3).reshape(e, P, fc * d)], axis=2),
        "b1_t": b1.reshape(e, fc, P).transpose(0, 2, 1),
        "b2": b2,
    }
    nc = bacc.Bacc("TRN2", target_bir_lowering=False, num_devices=1)
    args = {}
    for name, a in arrays.items():
        arrays[name] = a = np.ascontiguousarray(a)
        args[name] = nc.dram_tensor(name, a.shape, mybir.dt.from_np(a.dtype), kind="ExternalInput").ap()
    out = nc.dram_tensor("out", x.shape, F32, kind="ExternalOutput").ap()
    gnn_moe_kernel(nc, out=out, **args)
    return run_bass_kernel_spmd(nc, [arrays], core_ids=[0]).results[0]["out"]
```

```python
from contextlib import ExitStack

import concourse.bass as bass
from concourse import mybir

F32 = mybir.dt.float32
F32R = mybir.dt.float32r
BF16 = mybir.dt.bfloat16
I32 = mybir.dt.int32
U32 = mybir.dt.uint32
ALU = mybir.AluOpType
ACT = mybir.ActivationFunctionType
AX = mybir.AxisListType
Rows = bass.IndirectOffsetOnAxis

P = 128
EPS = 1e-5
TOPK = 2
SLOT = 2 * P
NOWHERE = 1 << 20


def gnn_moe_kernel(nc, x, adj_t, wn_t, ws_t, b_neigh, b_self, wg, bg, w12, b1_t, b2, out):
    N, D = x.shape
    E, F = b1_t.shape[0], b1_t.shape[1] * b1_t.shape[2]
    T = N // P
    DC = D // P
    FC = F // P
    G1 = D + 2
    HALF = N // 2
    WW = DC * F + FC * D
    WCH = WW // 4
    SLOTS = (TOPK * N + E * SLOT - 1) // SLOT
    NS = SLOTS + 1
    PAIR_ROWS = E * N + SLOT
    assert T % 2 == 0 and SLOTS % 2 == 1 and DC == 2 and FC % 2 == 0 and WCH == F

    z_rows = nc.dram_tensor("z_rows", (N, D), F32, kind="Internal").ap()
    pairs = nc.dram_tensor("pairs", (PAIR_ROWS, 4), F32, kind="Internal").ap()

    with ExitStack() as ctx:
        def sb(name, shape, dt=F32):
            return ctx.enter_context(nc.sbuf_tensor(name, shape, dt))

        def sem(name):
            return ctx.enter_context(nc.semaphore(name))

        def sems(name, n=2):
            return [sem(f"{name}{j}") for j in range(n)]

        ident = sb("ident", [P, P])
        upper = sb("upper", [P, P], BF16)
        ones = sb("ones", [P, P], BF16)
        iota_e = sb("iota_e", [P, E])
        tokens = sb("tokens", [P, T], I32)
        wg_sb = sb("wg_sb", [P, DC, E])
        bg_sb = sb("bg_sb", [P, E])
        bias_n = sb("bias_n", [P, D])
        bias_s = sb("bias_s", [P, D])
        bias = sb("bias", [P, D])
        x_sb = sb("x_sb", [P, T, D])
        self_sb = sb("self_sb", [P, T, D])
        stats = sb("stats", [P, T, 6])
        mv = sb("mv", [P, T, 2])
        ln = sb("ln", [P, 4, T])
        hn = sb("hn", [P, 2, D])
        adj_raw = sb("adj_raw", [P, 2, N])
        split = sb("split", [P, max(4 * WW, T * (G1 + D) + 4 * N)], F32R)
        zt = sb("zt", [P, 4 * D], F32R)
        x1 = sb("x1", [P, 2, D])
        xt = sb("xt", [P, D])
        z = sb("z", [P, 2, D])
        ztf = sb("ztf", [P, D])
        sm = sb("sm", [P, 16])
        lg = sb("lg", [P, E])
        top = sb("top", [P, 2, 8])
        top_i = sb("top_i", [P, 8], U32)
        hot = sb("hot", [P, TOPK, E])
        hot_pos = sb("hot_pos", [P, TOPK, E])
        mask = sb("mask", [P, E], BF16)
        base0 = sb("base0", [P, E])
        base = sb("base", [P, E])
        pos = sb("pos", [P, E])
        warm = sb("warm", [P, 2])
        slot_i = sb("slot_i", [P, 2, TOPK], I32)
        pair = sb("pair", [P, 2, TOPK, 4])
        fill = sb("fill", [P, PAIR_ROWS // P, 4])
        thr = sb("thr", [1, 8])
        tri = sb("tri", [1, E, E])
        iota_s = sb("iota_s", [1, NS])
        tb8 = sb("tb8", [1, 2, E, E])
        cnt = sb("cnt", [1, 3, E])
        ge = sb("ge", [1, 2, NS, E])
        tab_f = sb("tab_f", [1, 4, NS])
        tab = sb("tab", [1, 2, NS], I32)
        w_raw = sb("w_raw", [P, 2, WW])
        b1_sb = sb("b1_sb", [P, 2, FC])
        b2_sb = sb("b2_sb", [P, 2, D])
        slot_pair = sb("slot_pair", [P, 2, 2, 4])
        kept = sb("kept", [P, 2, 2], I32)
        zg = sb("zg", [P, 2, 2, D])
        h_raw = sb("h_raw", [P, 2, 2 * SLOT])
        h_hi = sb("h_hi", [P, FC, SLOT], F32R)
        h_lo = sb("h_lo", [P, FC, SLOT], F32R)
        ex = sb("ex", [P, 2, 2])
        den = sb("den", [P, 2])
        coef = sb("coef", [P, 2, 2])
        y_b = sb("y_b", [P, 2 * D])
        y_c = sb("y_c", [P, 2, 2, D])

        g_hi = split[:, 0:T * G1].rearrange("p (t c) -> p t c", c=G1)
        g_lo = split[:, T * G1:T * G1 + T * D].rearrange("p (t c) -> p t c", c=D)

        def adj_split(b, part):
            at = T * (G1 + D) + (2 * b + part) * N
            return split[:, at:at + N]

        def w_split(b, part):
            return split[:, (2 * b + part) * WW:(2 * b + part + 1) * WW]

        gw_raw = y_c[:].rearrange("p b j d -> p (b j d)").rearrange("p (c f) -> p c f", c=DC)
        gw_hi = h_hi[:, 0:FC // 2, :].rearrange("p a t -> p (a t)").rearrange("p (c f) -> p c f", c=DC)
        gw_lo = h_hi[:, FC // 2:FC, :].rearrange("p a t -> p (a t)").rearrange("p (c f) -> p c f", c=DC)

        bank = [ctx.enter_context(nc.psum_tensor(f"bank{j}", [P, 512], F32)) for j in range(8)]

        x_in = sems("x_in", 4)
        gw_in, bias_in = sem("gw_in"), sem("bias_in")
        consts = sem("consts")
        fill_ready = sem("fill_ready")
        ones_ready = sem("ones_ready")
        fill_out = sem("fill_out")
        dve_own = sem("dve_own")
        act_own = sem("act_own")
        var_all, std_all = sem("var_all"), sem("std_all")
        gw_split = sem("gw_split")
        hn_ready, ht_ps, ht_hi, ht_lo = sem("hn_ready"), sem("ht_ps"), sem("ht_hi"), sem("ht_lo")
        gs_ps, g_hi_ready, g_done = sem("gs_ps"), sem("g_hi_ready"), sem("g_done")
        adj_in = sems("adj_in")
        adj_hi, adj_lo = sem("adj_hi"), sem("adj_lo")
        acc_done, acc_read = sem("acc_done"), sem("acc_read")
        var_ready, std_ready, z_ready = sem("var_ready"), sem("std_ready"), sem("z_ready")
        x1_out, z_out = sems("x1_out"), sems("z_out")
        zt_r_ps, zt_r_sb, logit_ps = sem("zt_r_ps"), sem("zt_r_sb"), sem("logit_ps")
        mask_ready, rank_ps, slot_ready = sem("mask_ready"), sem("rank_ps"), sem("slot_ready")
        route = sem("route")
        place_own = sem("place_own")
        pair_ready = sem("pair_ready")
        pair_out = sems("pair_out")
        table_own = sem("table_own")
        table_ready = sem("table_ready")
        w_in, b_in, pair_in = sems("w_in"), sems("b_in"), sems("pair_in")
        w_hi_ready, w_lo_ready = sem("w_hi_ready"), sem("w_lo_ready")
        z_got = [sems(f"z_got{b}_") for b in range(2)]
        zt_ps, zt_hi_ready, zt_lo_ready = sem("zt_ps"), sem("zt_hi_ready"), sem("zt_lo_ready")
        hid_ps, hid_relu, hid_hi, hid_lo = sem("hid_ps"), sem("hid_relu"), sem("hid_hi"), sem("hid_lo")
        ex_ready, coef_step = sem("ex_ready"), sem("coef_step")
        y_ps, y_biased, y_ready = sem("y_ps"), sem("y_biased"), sem("y_ready")
        y_added = sems("y_added")
        idx_kept = sem("idx_kept")
        passed = {e: sem(f"passed_{e}") for e in ("sp", "pool", "dve")}

        NQ = FC // 2
        RELUS = [2 + 6 * (q // 2) + 4 * (q % 2) for q in range(NQ)]
        CHOICE = 4
        LN2 = 9

        def settle(eng, name):
            eng.sem_inc(passed[name], 1)

        with nc.Block() as block:

            @block.sync
            def _(sp):
                x_v = x.rearrange("(t p) d -> p t d", p=P)
                for j in range(4):
                    sp.dma_start(x_sb[:, 4 * j:4 * j + 4, :], x_v[:, 4 * j:4 * j + 4, :]).then_inc(x_in[j], 16)
                sp.dma_start(gw_raw[:, :, 0:D], wn_t.rearrange("(c p) f -> p c f", p=P)).then_inc(gw_in, 16)
                sp.dma_start(gw_raw[:, :, D:2 * D], ws_t.rearrange("(c p) f -> p c f", p=P)).then_inc(gw_in, 16)
                sp.dma_start(bias_n[:], b_neigh[None, :].to_broadcast([P, D])).then_inc(bias_in, 16)
                sp.dma_start(bias_s[:], b_self[None, :].to_broadcast([P, D])).then_inc(bias_in, 16)
                sp.dma_start(wg_sb[:], wg.rearrange("(c p) e -> p c e", p=P)).then_inc(bias_in, 16)
                sp.dma_start(bg_sb[:], bg[None, :].to_broadcast([P, E])).then_inc(bias_in, 16)
                for b in range(2):
                    sp.dma_start(adj_raw[:, b, :], adj_t[b]).then_inc(adj_in[b], 16)
                sp.wait_ge(fill_ready, 2)
                sp.dma_start(pairs.rearrange("(p r) w -> p r w", p=P), fill[:]).then_inc(fill_out, 16)
                sp.dma_start(w_raw[:, 0, :], w12[0]).then_inc(w_in[0], 16)
                sp.dma_start(b1_sb[:, 0, :], b1_t[0]).then_inc(b_in[0], 16)
                sp.dma_start(b2_sb[:, 0, :], b2[0:1, :].to_broadcast([P, D])).then_inc(b_in[0], 16)
                for b in range(2):
                    sp.wait_ge(adj_lo, 2 * b + 2)
                    sp.dma_start(adj_raw[:, b, :], adj_t[2 + b]).then_inc(adj_in[b], 16)

                def store(i, b):
                    sp.wait_ge(z_ready, i + 1)
                    sp.dma_start(out[bass.ds(i * P, P), :], x1[:, b, :]).then_inc(x1_out[b], 16)
                    sp.dma_start(z_rows[bass.ds(i * P, P), :], z[:, b, :]).then_inc(z_out[b], 16)

                with sp.Fori(0, T // 2 - 2) as k:
                    for b in range(2):
                        store(2 * k + b, b)
                        sp.wait_ge(adj_lo, 4 * k + 2 * b + 6)
                        sp.dma_start(adj_raw[:, b, :], adj_t[bass.ds(2 * k + b + 4, 1)].rearrange("a p n -> (a p) n")).then_inc(adj_in[b], 16)
                for i in range(T - 4, T):
                    store(i, i % 2)

                def load_pairs(b, at):
                    rows = pairs[bass.ds(at, SLOT), :].rearrange("(j p) w -> p j w", p=P)
                    sp.dma_start(slot_pair[:, b, :, :], rows).then_inc(pair_in[b], 16)

                def first_row(s):
                    return sp.value_load(tab[0:1, 1, bass.ds(s, 1)], min_val=0, max_val=E * N)

                def expert(s):
                    return sp.value_load(tab[0:1, 0, bass.ds(s, 1)], min_val=0, max_val=E - 1)

                def load_weights(b, e):
                    sp.dma_start(w_raw[:, b, :], w12[bass.ds(e, 1)].rearrange("a p n -> (a p) n")).then_inc(w_in[b], 16)

                def hold(s, value):
                    sp.wait_ge(s, value)
                    settle(sp, "sp")

                def ahead(s, b, two=True):
                    if two:
                        hold(w_lo_ready, 4 * s + 4)
                        load_weights(b, expert(s + 2))
                        hold(zt_ps, s + 1)
                        hold(idx_kept, s + 1)
                        hold(ex_ready, s + 1)
                        load_pairs(b, first_row(s + 2))
                    if not isinstance(s, int) or s >= 1:
                        hold(y_biased, s)
                    e = expert(s + 1)
                    sp.dma_start(b1_sb[:, 1 - b, :], b1_t[bass.ds(e, 1)].rearrange("a p n -> (a p) n")).then_inc(b_in[1 - b], 16)
                    sp.dma_start(b2_sb[:, 1 - b, :], b2[bass.ds(e, 1), :].to_broadcast([P, D])).then_inc(b_in[1 - b], 16)

                for c in range(TOPK):
                    sp.wait_ge(pair_out[c], 16 * T)
                load_pairs(0, 0)
                sp.wait_ge(table_ready, 1)
                load_pairs(1, first_row(1))
                load_weights(1, expert(1))
                for s in range(2):
                    ahead(s, s)
                with sp.Fori(1, (SLOTS - 3) // 2) as k:
                    for b in range(2):
                        ahead(2 * k + b, b)
                ahead(SLOTS - 3, 0)
                ahead(SLOTS - 2, 1, two=False)
                for j in range(2):
                    sp.wait_ge(y_added[j], 16 * SLOTS)
                    sp.wait_ge(x1_out[j], 16 * T // 2)

            @block.gpsimd
            def _(pool):
                pool.memset(ones[:], 1.0).then_inc(ones_ready, 1)
                pool.memset(ident[:], 0.0).then_inc(fill_ready, 1)
                pool.memset(upper[:], 1.0)
                pool.memset(fill[:], 0.0)
                pool.memset(pair[:], 0.0)
                pool.memset(zg[:], 0.0)
                pool.memset(tri[:], 1.0)
                pool.memset(g_hi[:, :, D:D + 1].bitcast(F32), 1.0)
                pool.memset(g_hi[:, :, D + 1:D + 2].bitcast(F32), 0.0)
                pool.iota(thr[:], [[SLOT, 8]], base=0, channel_multiplier=0, allow_small_or_imprecise_dtypes=True)
                pool.iota(iota_s[:], [[1, NS]], base=0, channel_multiplier=0, allow_small_or_imprecise_dtypes=True)
                pool.iota(iota_e[:], [[1, E]], base=0, channel_multiplier=0, allow_small_or_imprecise_dtypes=True)
                pool.iota(base0[:], [[N, E]], base=0, channel_multiplier=0, allow_small_or_imprecise_dtypes=True)
                pool.iota(base[:], [[N, E]], base=0, channel_multiplier=0, allow_small_or_imprecise_dtypes=True)
                pool.iota(tokens[:], [[P, T]], base=0, channel_multiplier=1).then_inc(consts, 1)
                pool.wait_ge(consts, 1)
                pool.memset(fill[:, :, 0:1].bitcast(I32), NOWHERE).then_inc(fill_ready, 1)
                pool.affine_select(ident[:], ident[:], [[-1, P]], ALU.not_equal, 1.0, base=0, channel_multiplier=1)
                pool.affine_select(upper[:], upper[:], [[1, P]], ALU.is_gt, 0.0, base=0, channel_multiplier=-1)
                pool.affine_select(tri[:], tri[:], [[1, E], [-1, E]], ALU.is_ge, 0.0, base=0, channel_multiplier=0)
                pool.memset(thr[:, 0:1], -1.0).then_inc(consts, 1)

                pool.wait_ge(fill_out, 16)

                def scatter(i, b):
                    pool.wait_ge(mask_ready, i + 1)
                    t0 = top[:, b, 0:1]
                    pool.tensor_copy(pair[:, b, :, 0:1].bitcast(I32), tokens[:, None, bass.ds(i, 1)].to_broadcast([P, TOPK, 1]))
                    pool.tensor_tensor(pair[:, b, :, 1], top[:, b, 1:2].to_broadcast([P, TOPK]), t0.to_broadcast([P, TOPK]), ALU.subtract)
                    pool.tensor_tensor(pair[:, b, :, 2], top[:, b, 0:TOPK], t0.to_broadcast([P, TOPK]), ALU.subtract).then_inc(pair_ready, 1)
                    pool.wait_ge(pair_ready, i + 1)
                    pool.wait_ge(slot_ready, i + 1)
                    settle(pool, "pool")
                    for c in range(TOPK):
                        pool.indirect_dma_start(pairs, Rows(slot_i[:, b, c:c + 1], 0), pair[:, b, c, :],
                                                None).then_inc(pair_out[c], 16)
                    for c in range(TOPK):
                        pool.wait_ge(pair_out[c], 16 * i + 16)
                    settle(pool, "pool")

                with pool.Fori(0, T // 2) as k:
                    for b in range(2):
                        scatter(2 * k + b, b)

                for b in range(2):
                    pool.wait_ge(z_out[b], 16 * T // 2)
                    pool.wait_ge(x1_out[b], 16 * T // 2)

                def gather(s, b, k):
                    pool.wait_ge(pair_in[b], 16 * k + 16)
                    if not isinstance(s, int) or s >= 2:
                        pool.wait_ge(zt_ps, s - 1)
                    settle(pool, "pool")
                    for j in range(2):
                        pool.indirect_dma_start(zg[:, b, j, :], None, z_rows, Rows(slot_pair[:, b, j, 0:1].bitcast(I32), 0),
                                                bounds_check=N - 1, oob_is_err=False).then_inc(z_got[b][j], 16)

                def add(s, b):
                    pool.wait_ge(y_ready, 2 * s + 2)
                    settle(pool, "pool")
                    for j in range(2):
                        pool.indirect_dma_start(out, Rows(kept[:, b, j:j + 1], 0), y_c[:, b, j, :], None,
                                                bounds_check=N - 1, oob_is_err=False,
                                                compute_op=ALU.add).then_inc(y_added[j], 16)
                    for j in range(2):
                        pool.wait_ge(y_added[j], 16 * s + 16)
                    settle(pool, "pool")

                def keep(b):
                    pool.tensor_copy(kept[:, b, :, None], slot_pair[:, b, :, 0:1].bitcast(I32)).then_inc(idx_kept, 1)

                for b in range(2):
                    gather(b, b, 0)
                    keep(b)

                def turn(s, b, k, more=True):
                    if more:
                        gather(s + 2, b, k + 1)
                    pool.wait_ge(idx_kept, s + 1)
                    add(s, b)
                    if more:
                        keep(b)

                with pool.Fori(0, (SLOTS - 3) // 2) as k:
                    for b in range(2):
                        turn(2 * k + b, b, k)
                turn(SLOTS - 3, 0, (SLOTS - 3) // 2)
                turn(SLOTS - 2, 1, 0, more=False)
                turn(SLOTS - 1, 0, 0, more=False)

            @block.scalar
            def _(act):
                act.wait_ge(ones_ready, 1)
                act.activation(warm[:, 0:1], ones[:, 0:1], ACT.Sqrt)
                act.wait_ge(gw_in, 32)
                act.activation(gw_hi[:], gw_raw[:], ACT.Copy).then_inc(gw_split, 1)
                act.wait_ge(var_all, 1)
                act.activation(ln[:, 1, :], ln[:, 0, :], ACT.Sqrt).then_inc(std_all, 1)

                def rows_high(i, b):
                    act.wait_ge(ht_ps, i + 1)
                    act.activation(zt[:, 2 * D * b:2 * D * b + D], bank[b][:, 0:D], ACT.Copy).then_inc(ht_hi, 1)

                def features_high(i, b):
                    act.wait_ge(gs_ps, i + 1)
                    act.activation(g_hi[:, bass.ds(i, 1), 0:D], bank[2 + b][:, None, 0:D], ACT.Copy).then_inc(g_hi_ready, 1)

                rows_high(0, 0)
                with act.Fori(0, T // 2 - 1) as k:
                    for b in range(2):
                        rows_high(2 * k + b + 1, 1 - b)
                        features_high(2 * k + b, b)
                rows_high(T - 1, 1)
                for i in (T - 2, T - 1):
                    features_high(i, i % 2)

                def high(i, b, half, k):
                    act.wait_ge(adj_in[b], 16 * k + 16)
                    cols = slice(half * HALF, half * HALF + HALF)
                    act.activation(adj_split(b, 0)[:, cols], adj_raw[:, b, cols], ACT.Copy).then_inc(adj_hi, 1)

                def root(i):
                    act.wait_ge(var_ready, i + 1)
                    act.activation(sm[:, 4:5], sm[:, 3:4], ACT.Sqrt).then_inc(std_ready, 1)

                def logits_in(i):
                    act.wait_ge(zt_r_ps, i + 1)
                    act.activation(ztf[:], bank[6][:, 0:D], ACT.Copy).then_inc(zt_r_sb, 1)

                for b in range(2):
                    for half in range(2):
                        high(b, b, half, 0)
                with act.Fori(0, T // 2 - 1) as k:
                    for b in range(2):
                        i = 2 * k + b
                        act.wait_ge(acc_done, i + 1)
                        high(i + 2, b, 0, k + 1)
                        root(i)
                        high(i + 2, b, 1, k + 1)
                        logits_in(i)
                for i in (T - 2, T - 1):
                    root(i)
                    logits_in(i)
                act.activation(warm[:, 1:2], ones[:, 0:1], ACT.Exp)

                def high_w(b, c, k):
                    act.wait_ge(w_in[b], 16 * k + 16)
                    cols = slice(c * WCH, c * WCH + WCH)
                    act.activation(w_split(b, 0)[:, cols], w_raw[:, b, cols], ACT.Copy).then_inc(w_hi_ready, 1)

                def high_z(s):
                    act.wait_ge(zt_ps, s + 1)
                    act.activation(zt[:, 0:2 * D], bank[6][:], ACT.Copy).then_inc(zt_hi_ready, 1)

                def slot(s, b, k, more=True):
                    act.wait_ge(pair_in[b], 16 * k + 16)
                    if not isinstance(s, int) or s >= 1:
                        act.wait_ge(coef_step, 3 * s)
                    act.activation(ex[:], slot_pair[:, b, :, 1:3], ACT.Exp).then_inc(ex_ready, 1)
                    act.wait_ge(b_in[b], 32 * k + 32)
                    if more:
                        act.wait_ge(y_ps, s)
                    for q in range(NQ):
                        act.wait_ge(hid_ps, NQ * s + q + 1)
                        if not isinstance(s, int) or s > 0 or q >= 2:
                            act.wait_ge(hid_lo, NQ * s + q - 1)
                        for c in range(2):
                            act.activation(h_raw[:, q % 2, c * SLOT:c * SLOT + SLOT], bank[2 + q][:, c * SLOT:c * SLOT + SLOT],
                                           ACT.Relu, bias=b1_sb[:, b, 2 * q + c:2 * q + c + 1]).then_inc(hid_relu, 1)
                            if q % 2:
                                act.activation(h_hi[:, 2 * q + c, :], bank[2 + q][:, c * SLOT:c * SLOT + SLOT],
                                               ACT.Relu, bias=b1_sb[:, b, 2 * q + c:2 * q + c + 1]).then_inc(hid_relu, 1)
                        if q == 0 and (not isinstance(s, int) or s >= 1):
                            results(s - 1, 1 - b)
                    if more:
                        high_w(1 - b, 0, k + b)
                        high_w(1 - b, 1, k + b)
                        high_z(s + 1)
                        high_w(1 - b, 2, k + b)
                        high_w(1 - b, 3, k + b)

                def results(s, b):
                    act.wait_ge(y_biased, s + 1)
                    act.wait_ge(coef_step, 3 * s + 3)
                    if not isinstance(s, int) or s >= 2:
                        act.wait_ge(y_added[0], 16 * s - 16)
                        act.wait_ge(y_added[1], 16 * s - 16)
                    for j in range(2):
                        act.activation(y_c[:, b, j, :], y_b[:, j * D:j * D + D], ACT.Copy,
                                       scale=coef[:, b, j:j + 1]).then_inc(y_ready, 1)

                act.wait_ge(acc_done, T)
                for c in range(4):
                    high_w(0, c, 0)
                high_z(0)
                for s in range(2):
                    slot(s, s, 0)
                with act.Fori(1, SLOTS // 2) as k:
                    for b in range(2):
                        slot(2 * k + b, b, k)
                slot(SLOTS - 1, 0, SLOTS // 2, more=False)
                results(SLOTS - 1, 0)

            @block.vector
            def _(dve):
                own = [0]

                def link(ins):
                    own[0] += 1
                    ins.then_inc(dve_own, 1)
                    dve.wait_ge(dve_own, own[0])

                for j in range(4):
                    dve.wait_ge(x_in[j], 16)
                    for t in range(4 * j, 4 * j + 4):
                        last = dve.bn_stats(stats[:, t, :], x_sb[:, t, :])
                link(last)
                for t in range(T):
                    last = dve.bn_aggr(mv[:, t, :], stats[:, t, :])
                link(last)
                dve.tensor_scalar(ln[:, 0, :], mv[:, :, 1], EPS, None, ALU.add).then_inc(var_all, 1)
                dve.wait_ge(std_all, 1)
                link(dve.reciprocal(ln[:, 1, :], ln[:, 1, :]))
                link(dve.tensor_tensor(ln[:, 2, :], ln[:, 0, :], ln[:, 1, :], ALU.mult))
                link(dve.tensor_tensor(ln[:, 2, :], ln[:, 2, :], ln[:, 1, :], ALU.mult))
                link(dve.tensor_scalar(ln[:, 2, :], ln[:, 2, :], -0.5, 1.5, ALU.mult, ALU.add))
                link(dve.tensor_tensor(ln[:, 3, :], ln[:, 1, :], ln[:, 2, :], ALU.mult))

                def normed(i, b):
                    dve.tensor_scalar(hn[:, b, None, :], x_sb[:, bass.ds(i, 1), :], mv[:, bass.ds(i, 1), 0], ln[:, 3, bass.ds(i, 1)],
                                      ALU.subtract, ALU.mult).then_inc(hn_ready, 1)

                normed(0, 0)
                normed(1, 1)
                dve.wait_ge(gw_split, 1)
                dve.tensor_tensor(gw_lo[:], gw_raw[:], gw_hi[:], ALU.subtract).then_inc(gw_split, 1)
                dve.wait_ge(bias_in, 64)
                link(dve.tensor_tensor(bias[:], bias_n[:], bias_s[:], ALU.add))

                def rows_low(i, b, more=True):
                    dve.wait_ge(ht_hi, i + 1)
                    dve.tensor_tensor(zt[:, 2 * D * b + D:2 * D * b + 2 * D], bank[b][:, 0:D], zt[:, 2 * D * b:2 * D * b + D],
                                      ALU.subtract).then_inc(ht_lo, 1)
                    if more:
                        normed(i + 2, b)

                def features(i, b):
                    dve.wait_ge(g_hi_ready, i + 1)
                    dve.tensor_tensor(g_lo[:, bass.ds(i, 1), :], bank[2 + b][:, None, 0:D], g_hi[:, bass.ds(i, 1), 0:D],
                                      ALU.subtract)
                    dve.tensor_tensor(self_sb[:, bass.ds(i, 1), :], bank[2 + b][:, None, D:2 * D], bias[:, None, :],
                                      ALU.add).then_inc(g_done, 1)

                rows_low(0, 0)
                with dve.Fori(0, T // 2 - 2) as k:
                    for b in range(2):
                        rows_low(2 * k + b + 1, 1 - b)
                        features(2 * k + b, b)
                for i in range(T - 4, T):
                    if i + 1 < T:
                        rows_low(i + 1, (i + 1) % 2, more=i + 3 < T)
                    features(i, i % 2)

                def low(i, b, half, k):
                    dve.wait_ge(adj_hi, 2 * i + half + 1)
                    cols = slice(half * HALF, half * HALF + HALF)
                    dve.tensor_tensor(adj_split(b, 1)[:, cols], adj_raw[:, b, cols], adj_split(b, 0)[:, cols],
                                      ALU.subtract).then_inc(adj_lo, 1)

                first = own[0]
                for b in range(2):
                    for half in range(2):
                        low(b, b, half, 0)
                dve.wait_ge(g_done, T)
                dve.wait_ge(consts, 2)

                def residual(i, b, k, choose=True):
                    n = [0, 0]

                    def step(ins, s):
                        n[s] += 1
                        ins.then_inc((dve_own, route)[s], 1)

                    def after(s, plain=False):
                        dve.wait_ge((dve_own, route)[s], (LN2 * i + first if s == 0 else CHOICE * (i - 1)) + n[s])
                        if plain:
                            settle(dve, "dve")

                    dve.wait_ge(acc_done, i + 1)
                    step(dve.tensor_scalar(sm[:, 0:1], bank[b][:, D:D + 1], EPS, None, ALU.add), 0)
                    if choose:
                        dve.wait_ge(logit_ps, i)
                        step(dve.tensor_tensor(lg[:], bank[7][:, 0:E], bg_sb[:], ALU.add), 1)
                    after(0)
                    step(dve.reciprocal(sm[:, 1:2], sm[:, 0:1]), 0)
                    if choose:
                        if not isinstance(i, int) or i >= 3:
                            dve.wait_ge(pair_ready, i - 2)
                        after(1, plain=True)
                        step(dve.max(top[:, 1 - b, :], lg[:]), 1)
                    after(0)
                    dve.scalar_tensor_tensor(out=xt[:, None, :], in0=bank[b][:, None, 0:D], scalar=sm[:, 1:2],
                                             in1=self_sb[:, bass.ds(i, 1), :], op0=ALU.mult, op1=ALU.add).then_inc(acc_read, 1)
                    if choose:
                        after(1, plain=True)
                        step(dve.max_index(top_i[:], top[:, 1 - b, :], lg[:]), 1)
                    dve.wait_ge(acc_read, i + 1)
                    dve.wait_ge(x1_out[b], 16 * k)
                    dve.wait_ge(z_out[b], 16 * k)
                    step(dve.scalar_tensor_tensor(out=x1[:, b, None, :], in0=xt[:, None, :], scalar=0.0, in1=x_sb[:, bass.ds(i, 1), :],
                                                  op0=ALU.max, op1=ALU.add), 0)
                    if choose:
                        after(1)
                        step(dve.tensor_tensor(hot[:], iota_e[:, None, :].to_broadcast([P, TOPK, E]),
                                               top_i[:, 0:TOPK, None].to_broadcast([P, TOPK, E]), ALU.is_equal), 1)
                    after(0)
                    step(dve.bn_stats(stats[:, 0, :], x1[:, b, :]), 0)
                    if choose:
                        after(1)
                        dve.tensor_tensor(mask[:], hot[:, 0, :], hot[:, 1, :], ALU.add).then_inc(mask_ready, 1)
                    after(0, plain=True)
                    step(dve.bn_aggr(mv[:, 0, :], stats[:, 0, :]), 0)
                    after(0)
                    dve.tensor_scalar(sm[:, 3:4], mv[:, 0, 1:2], EPS, None, ALU.add).then_inc(var_ready, 1)
                    dve.wait_ge(std_ready, i + 1)
                    step(dve.reciprocal(sm[:, 5:6], sm[:, 4:5]), 0)
                    after(0)
                    step(dve.scalar_tensor_tensor(out=sm[:, 6:7], in0=sm[:, 5:6], scalar=sm[:, 3:4], in1=sm[:, 5:6],
                                                  op0=ALU.mult, op1=ALU.mult), 0)
                    after(0)
                    step(dve.tensor_scalar(sm[:, 7:8], sm[:, 6:7], -0.5, 1.5, ALU.mult, ALU.add), 0)
                    after(0)
                    step(dve.tensor_tensor(sm[:, 8:9], sm[:, 5:6], sm[:, 7:8], ALU.mult), 0)
                    after(0)
                    dve.tensor_scalar(z[:, b, :], x1[:, b, :], mv[:, 0, 0:1], sm[:, 8:9], ALU.subtract,
                                      ALU.mult).then_inc(z_ready, 1)
                    assert n[0] == LN2 and n[1] in (0, CHOICE)

                def place(i, b):
                    dve.wait_ge(rank_ps, i + 1)
                    dve.tensor_tensor(pos[:], bank[5][:, 0:E], base[:], ALU.add).then_inc(place_own, 1)
                    dve.tensor_tensor(base[:], bank[5][:, E:2 * E], base[:], ALU.add)
                    dve.wait_ge(place_own, 2 * i + 1)
                    dve.tensor_tensor(hot_pos[:], hot[:], pos[:, None, :].to_broadcast([P, TOPK, E]), ALU.mult).then_inc(place_own, 1)
                    dve.wait_ge(place_own, 2 * i + 2)
                    if not isinstance(i, int) or i >= 2:
                        for c in range(TOPK):
                            dve.wait_ge(pair_out[c], 16 * i - 16)
                    with nc.allow_low_precision(reason="row numbers, exact in float32 and as integers"):
                        dve.tensor_reduce(slot_i[:, b, :], hot_pos[:], AX.X, ALU.add).then_inc(slot_ready, 1)

                residual(0, 0, 0, choose=False)
                for half in range(2):
                    low(2, 0, half, 1)
                residual(1, 1, 0)
                low(3, 1, 0, 1)
                place(0, 0)
                low(3, 1, 1, 1)
                with dve.Fori(1, T // 2 - 1) as k:
                    for b in range(2):
                        i = 2 * k + b
                        residual(i, b, k)
                        low(i + 2, b, 0, k + 1)
                        place(i - 1, 1 - b)
                        low(i + 2, b, 1, k + 1)
                for i in (T - 2, T - 1):
                    residual(i, i % 2, T // 2 - 1)
                    place(i - 1, (i - 1) % 2)
                i, c0 = T - 1, CHOICE * (T - 1)
                dve.wait_ge(logit_ps, T)
                dve.tensor_tensor(lg[:], bank[7][:, 0:E], bg_sb[:], ALU.add).then_inc(route, 1)
                dve.wait_ge(route, c0 + 1)
                dve.wait_ge(pair_ready, T - 2)
                dve.max(top[:, 1, :], lg[:]).then_inc(route, 1)
                dve.wait_ge(route, c0 + 2)
                dve.max_index(top_i[:], top[:, 1, :], lg[:]).then_inc(route, 1)
                dve.wait_ge(route, c0 + 3)
                dve.tensor_tensor(hot[:], iota_e[:, None, :].to_broadcast([P, TOPK, E]),
                                  top_i[:, 0:TOPK, None].to_broadcast([P, TOPK, E]), ALU.is_equal).then_inc(route, 1)
                dve.wait_ge(route, c0 + 4)
                dve.tensor_tensor(mask[:], hot[:, 0, :], hot[:, 1, :], ALU.add).then_inc(mask_ready, 1)
                place(T - 1, 1)

                tn = [0]

                def tlink(ins):
                    tn[0] += 1
                    ins.then_inc(table_own, 1)
                    dve.wait_ge(table_own, tn[0])

                r0 = slice(0, 1)
                dve.wait_ge(slot_ready, T)
                tlink(dve.tensor_tensor(cnt[:, 0, :], base[r0, :], base0[r0, :], ALU.subtract))
                tlink(dve.tensor_tensor(tb8[:, 0], cnt[:, 0, :, None].to_broadcast([1, E, E]), thr[:, None, :].to_broadcast([1, E, 8]), ALU.is_gt))
                tlink(dve.tensor_reduce(cnt[:, 1, :], tb8[:, 0], AX.X, ALU.add))
                tlink(dve.tensor_tensor(tb8[:, 1], tri[:], cnt[:, 1, None, :].to_broadcast([1, E, E]), ALU.mult))
                tlink(dve.tensor_reduce(cnt[:, 2, :], tb8[:, 1], AX.X, ALU.add))
                tlink(dve.tensor_tensor(ge[:, 0], iota_s[:, :, None].to_broadcast([1, NS, E]), cnt[:, 2, None, :].to_broadcast([1, NS, E]), ALU.is_ge))
                dve.tensor_reduce(tab_f[:, 0, :], ge[:, 0], AX.X, ALU.add)
                tlink(dve.tensor_tensor(ge[:, 1], ge[:, 0], cnt[:, 1, None, :].to_broadcast([1, NS, E]), ALU.mult))
                tlink(dve.tensor_reduce(tab_f[:, 1, :], ge[:, 1], AX.X, ALU.add))
                tlink(dve.tensor_tensor(tab_f[:, 2, :], iota_s[:], tab_f[:, 1, :], ALU.subtract))
                tlink(dve.tensor_scalar(tab_f[:, 2, :], tab_f[:, 2, :], float(SLOT), None, ALU.mult))
                tlink(dve.scalar_tensor_tensor(out=tab_f[:, 3, :], in0=tab_f[:, 0, :], scalar=float(N), in1=tab_f[:, 2, :],
                                               op0=ALU.mult, op1=ALU.add))
                dve.tensor_scalar(tab[:, 0, :], tab_f[:, 0, :], float(E - 1), None, ALU.min)
                dve.tensor_scalar(tab[:, 1, :], tab_f[:, 3, :], float(E * N), None, ALU.min).then_inc(table_ready, 1)

                def low_w(b, c, s):
                    dve.wait_ge(w_hi_ready, 4 * s + c + 1)
                    cols = slice(c * WCH, c * WCH + WCH)
                    dve.tensor_tensor(w_split(b, 1)[:, cols], w_raw[:, b, cols], w_split(b, 0)[:, cols],
                                      ALU.subtract).then_inc(w_lo_ready, 1)

                def low_z(s):
                    dve.wait_ge(zt_hi_ready, s + 1)
                    dve.tensor_tensor(zt[:, 2 * D:4 * D], bank[6][:], zt[:, 0:2 * D], ALU.subtract).then_inc(zt_lo_ready, 1)

                def slot(s, b, k, more=True):
                    dve.wait_ge(ex_ready, s + 1)
                    if not isinstance(s, int) or s >= 2:
                        dve.wait_ge(y_ready, 2 * s - 2)
                    dve.tensor_scalar(den[:], ex[:, :, 0], 1.0, None, ALU.add).then_inc(coef_step, 1)
                    dve.wait_ge(coef_step, 3 * s + 1)
                    dve.reciprocal(den[:], den[:]).then_inc(coef_step, 1)
                    dve.wait_ge(coef_step, 3 * s + 2)
                    dve.tensor_tensor(coef[:, b, :], den[:], ex[:, :, 1], ALU.mult).then_inc(coef_step, 1)
                    for q in range(NQ):
                        dve.wait_ge(hid_relu, RELUS[-1] * s + RELUS[q])
                        raw = h_raw[:, q % 2, :]
                        hi = h_hi[:, 2 * q:2 * q + 2, :].rearrange("p a t -> p (a t)")
                        if q % 2 == 0:
                            dve.tensor_copy(hi, raw).then_inc(hid_hi, 1)
                            dve.wait_ge(hid_hi, NQ // 2 * s + q // 2 + 1)
                        dve.tensor_tensor(h_lo[:, 2 * q:2 * q + 2, :].rearrange("p a t -> p (a t)"), raw, hi,
                                          ALU.subtract).then_inc(hid_lo, 1)
                    if more:
                        low_w(1 - b, 0, s + 1)
                        low_w(1 - b, 1, s + 1)
                        low_z(s + 1)
                        low_w(1 - b, 2, s + 1)
                        low_w(1 - b, 3, s + 1)
                    dve.wait_ge(y_ps, s + 1)
                    if not isinstance(s, int) or s >= 1:
                        dve.wait_ge(y_ready, 2 * s)
                    dve.tensor_tensor(y_b[:].rearrange("p (j d) -> p j d", j=2), bank[b][:].rearrange("p (j d) -> p j d", j=2),
                                      b2_sb[:, b, None, :].to_broadcast([P, 2, D]), ALU.add).then_inc(y_biased, 1)

                for c in range(4):
                    low_w(0, c, 0)
                low_z(0)
                for s in range(2):
                    slot(s, s, 0)
                with dve.Fori(1, SLOTS // 2) as k:
                    for b in range(2):
                        slot(2 * k + b, b, k)
                slot(SLOTS - 1, 0, SLOTS // 2, more=False)

            @block.tensor
            def _(pe):
                pe.wait_ge(consts, 2)

                def rows_t(i, b):
                    pe.wait_ge(hn_ready, i + 1)
                    if not isinstance(i, int) or i >= 2:
                        pe.wait_ge(ht_lo, i - 1)
                    for c in range(DC):
                        last = pe.transpose(bank[b][:, c * P:c * P + P], hn[:, b, c * P:c * P + P], ident[:])
                    last.then_inc(ht_ps, 1)

                def products(out_ap, terms):
                    for n, (o, w, m) in enumerate(terms):
                        last = pe.matmul(o, w, m, start=(n == 0), stop=(n == len(terms) - 1), skip_group_check=True)
                    return last

                def features(i, b):
                    pe.wait_ge(ht_lo, i + 1)
                    if not isinstance(i, int) or i >= 2:
                        pe.wait_ge(g_done, i - 1)
                    hi, lo = zt[:, 2 * D * b:2 * D * b + D], zt[:, 2 * D * b + D:2 * D * b + 2 * D]
                    terms = []
                    for c in range(DC):
                        cc = slice(c * P, c * P + P)
                        terms += [(bank[2 + b][:], hi[:, cc], gw_hi[:, c, :]), (bank[2 + b][:], hi[:, cc], gw_lo[:, c, :]),
                                  (bank[2 + b][:], lo[:, cc], gw_hi[:, c, :])]
                    products(None, terms).then_inc(gs_ps, 1)

                pe.wait_ge(gw_split, 2)
                rows_t(0, 0)
                rows_t(1, 1)
                for i in range(2):
                    features(i, i)
                    rows_t(i + 2, i)
                with pe.Fori(1, T // 2 - 1) as k:
                    for b in range(2):
                        features(2 * k + b, b)
                        rows_t(2 * k + b + 2, b)
                for i in (T - 2, T - 1):
                    features(i, i % 2)

                def aggregate(b, j0, j1):
                    hi, lo = adj_split(b, 0), adj_split(b, 1)
                    for j in range(j0, j1):
                        jj = slice(j * P, j * P + P)
                        pe.matmul(bank[b][:, 0:G1], hi[:, jj], g_hi[:, j, :], start=(j == 0), stop=False, skip_group_check=True)
                        pe.matmul(bank[b][:, 0:D], hi[:, jj], g_lo[:, j, :], start=False, stop=False, skip_group_check=True)
                        last = pe.matmul(bank[b][:, 0:G1], lo[:, jj], g_hi[:, j, :], start=False, stop=(j == T - 1),
                                         skip_group_check=True)
                    return last

                def transpose_z(i, b):
                    pe.wait_ge(z_ready, i + 1)
                    if not isinstance(i, int) or i >= 1:
                        pe.wait_ge(zt_r_sb, i)
                    for c in range(DC):
                        last = pe.transpose(bank[6][:, c * P:c * P + P], z[:, b, c * P:c * P + P], ident[:])
                    last.then_inc(zt_r_ps, 1)

                def logits(i):
                    pe.wait_ge(zt_r_sb, i + 1)
                    if not isinstance(i, int) or i >= 1:
                        pe.wait_ge(mask_ready, i)
                    for c in range(DC):
                        last = pe.matmul(bank[7][:, 0:E], ztf[:, c * P:c * P + P], wg_sb[:, c, :], start=(c == 0), stop=(c == DC - 1))
                    last.then_inc(logit_ps, 1)

                def ranks(i):
                    pe.wait_ge(mask_ready, i + 1)
                    if not isinstance(i, int) or i >= 1:
                        pe.wait_ge(slot_ready, i)
                    pe.matmul(bank[5][:, 0:E], upper[:], mask[:], start=True, stop=True)
                    pe.matmul(bank[5][:, E:2 * E], ones[:], mask[:], start=True, stop=True).then_inc(rank_ps, 1)

                def tile(i, b, last=True, before=True):
                    pe.wait_ge(adj_lo, 2 * i + 1)
                    if before:
                        pe.wait_ge(acc_read, i - 1)
                    aggregate(b, 0, T // 2)
                    if before:
                        ranks(i - 2)
                    pe.wait_ge(adj_lo, 2 * i + 2)
                    aggregate(b, T // 2, 3 * T // 4)
                    if last:
                        transpose_z(i - 1, 1 - b)
                    aggregate(b, 3 * T // 4, T).then_inc(acc_done, 1)
                    if last:
                        logits(i - 1)

                pe.wait_ge(g_done, T)
                tile(0, 0, last=False, before=False)
                tile(1, 1, before=False)
                with pe.Fori(1, T // 2) as k:
                    for b in range(2):
                        tile(2 * k + b, b)
                ranks(T - 2)
                transpose_z(T - 1, 1)
                logits(T - 1)
                ranks(T - 1)

                def transpose_slot(s, b, k):
                    for j in range(2):
                        pe.wait_ge(z_got[b][j], 16 * k + 16)
                    if not isinstance(s, int) or s >= 1:
                        pe.wait_ge(zt_lo_ready, s)
                    for j in range(2):
                        for c in range(DC):
                            last = pe.transpose(bank[6][:, c * SLOT + j * P:c * SLOT + j * P + P], zg[:, b, j, c * P:c * P + P], ident[:])
                    last.then_inc(zt_ps, 1)

                def slot(s, b, k, more=True):
                    w_hi, w_lo = w_split(b, 0), w_split(b, 1)
                    z_hi, z_lo = zt[:, 0:2 * D], zt[:, 2 * D:4 * D]
                    pe.wait_ge(zt_lo_ready, s + 1)
                    pe.wait_ge(w_lo_ready, 4 * s + 2)
                    for q in range(NQ):
                        if not isinstance(s, int) or s >= 1:
                            pe.wait_ge(hid_relu, RELUS[-1] * (s - 1) + RELUS[q])
                        for c in range(2):
                            o = bank[2 + q][:, c * SLOT:c * SLOT + SLOT]
                            terms = []
                            for d in range(DC):
                                f = slice(d * F + (2 * q + c) * P, d * F + (2 * q + c) * P + P)
                                t = slice(d * SLOT, d * SLOT + SLOT)
                                terms += [(o, w_hi[:, f], z_hi[:, t]), (o, w_hi[:, f], z_lo[:, t]), (o, w_lo[:, f], z_hi[:, t])]
                            last = products(o, terms)
                        last.then_inc(hid_ps, 1)
                    if more:
                        transpose_slot(s + 1, 1 - b, k + b)
                    pe.wait_ge(w_lo_ready, 4 * s + 4)
                    if not isinstance(s, int) or s >= 2:
                        pe.wait_ge(y_biased, s - 1)
                    for j in range(2):
                        o = bank[b][:, j * D:j * D + D]
                        t = slice(j * P, j * P + P)
                        for c in range(FC):
                            if j == 0 and c % 2 == 0:
                                pe.wait_ge(hid_lo, NQ * s + c // 2 + 1)
                            d = slice(DC * F + c * D, DC * F + c * D + D)
                            pe.matmul(o, h_hi[:, c, t], w_hi[:, d], start=(c == 0), stop=False, skip_group_check=True)
                            pe.matmul(o, h_hi[:, c, t], w_lo[:, d], start=False, stop=False, skip_group_check=True)
                            last = pe.matmul(o, h_lo[:, c, t], w_hi[:, d], start=False, stop=(c == FC - 1), skip_group_check=True)
                    last.then_inc(y_ps, 1)

                transpose_slot(0, 0, 0)
                for s in range(2):
                    slot(s, s, 0)
                with pe.Fori(1, SLOTS // 2) as k:
                    for b in range(2):
                        slot(2 * k + b, b, k)
                slot(SLOTS - 1, 0, SLOTS // 2, more=False)


def kernel(x, adj, L0_gnn_W_neigh, L0_gnn_b_neigh, L0_gnn_W_self, L0_gnn_b_self, L0_ffn_Wg, L0_ffn_bg,
           L0_ffn_W1, L0_ffn_b1, L0_ffn_W2, L0_ffn_b2):
    import numpy as np
    import concourse.bacc as bacc
    from concourse.bass_utils import run_bass_kernel_spmd

    x, adj, w1, b1, w2, b2 = (np.asarray(a) for a in (x, adj, L0_ffn_W1, L0_ffn_b1, L0_ffn_W2, L0_ffn_b2))
    n, (e, d, f) = x.shape[0], w1.shape
    t, dc, fc = n // P, d // P, f // P
    arrays = {
        "x": x,
        "adj_t": adj.reshape(t, P, t, P).transpose(0, 3, 2, 1).reshape(t, P, n),
        "wn_t": np.asarray(L0_gnn_W_neigh).T,
        "ws_t": np.asarray(L0_gnn_W_self).T,
        "b_neigh": np.asarray(L0_gnn_b_neigh),
        "b_self": np.asarray(L0_gnn_b_self),
        "wg": np.asarray(L0_ffn_Wg),
        "bg": np.asarray(L0_ffn_bg),
        "w12": np.concatenate([w1.reshape(e, dc, P, f).transpose(0, 2, 1, 3).reshape(e, P, dc * f),
                               w2.reshape(e, fc, P, d).transpose(0, 2, 1, 3).reshape(e, P, fc * d)], axis=2),
        "b1_t": b1.reshape(e, fc, P).transpose(0, 2, 1),
        "b2": b2,
    }
    nc = bacc.Bacc("TRN2", target_bir_lowering=False, num_devices=1)
    args = {}
    for name, a in arrays.items():
        arrays[name] = a = np.ascontiguousarray(a)
        args[name] = nc.dram_tensor(name, a.shape, mybir.dt.from_np(a.dtype), kind="ExternalInput").ap()
    out = nc.dram_tensor("out", x.shape, F32, kind="ExternalOutput").ap()
    gnn_moe_kernel(nc, out=out, **args)
    return run_bass_kernel_spmd(nc, [arrays], core_ids=[0]).results[0]["out"]
```

```python
from contextlib import ExitStack

import concourse.bass as bass
from concourse import mybir

F32 = mybir.dt.float32
F32R = mybir.dt.float32r
BF16 = mybir.dt.bfloat16
I32 = mybir.dt.int32
U32 = mybir.dt.uint32
ALU = mybir.AluOpType
ACT = mybir.ActivationFunctionType
AX = mybir.AxisListType
Rows = bass.IndirectOffsetOnAxis

P = 128
EPS = 1e-5
TOPK = 2
SLOT = 2 * P
NOWHERE = 1 << 20


def gnn_moe_kernel(nc, x, adj_t, wn_t, ws_t, b_neigh, b_self, wg, bg, w12, b1_t, b2, out):
    N, D = x.shape
    E, F = b1_t.shape[0], b1_t.shape[1] * b1_t.shape[2]
    T = N // P
    DC = D // P
    FC = F // P
    G1 = D + 2
    HALF = N // 2
    WW = DC * F + FC * D
    WCH = WW // 4
    SLOTS = (TOPK * N + E * SLOT - 1) // SLOT
    TURNS = (SLOTS + 1) // 2
    NS = 2 * TURNS + 2
    PAIR_ROWS = E * N + SLOT
    assert T % 2 == 0 and DC == 2 and FC % 2 == 0 and WCH == F

    z_rows = nc.dram_tensor("z_rows", (N, D), F32, kind="Internal").ap()
    pairs = nc.dram_tensor("pairs", (PAIR_ROWS, 4), F32, kind="Internal").ap()

    with ExitStack() as ctx:
        def sb(name, shape, dt=F32):
            return ctx.enter_context(nc.sbuf_tensor(name, shape, dt))

        def sem(name):
            return ctx.enter_context(nc.semaphore(name))

        def sems(name, n=2):
            return [sem(f"{name}{j}") for j in range(n)]

        ident = sb("ident", [P, P])
        upper = sb("upper", [P, P], BF16)
        ones = sb("ones", [P, P], BF16)
        iota_e = sb("iota_e", [P, E])
        tokens = sb("tokens", [P, T], I32)
        wg_sb = sb("wg_sb", [P, DC, E])
        bg_sb = sb("bg_sb", [P, E])
        bias_n = sb("bias_n", [P, D])
        bias_s = sb("bias_s", [P, D])
        bias = sb("bias", [P, D])
        x_sb = sb("x_sb", [P, T, D])
        self_sb = sb("self_sb", [P, T, D])
        stats = sb("stats", [P, T, 6])
        mv = sb("mv", [P, T, 2])
        ln = sb("ln", [P, 4, T])
        hn = sb("hn", [P, 2, D])
        adj_raw = sb("adj_raw", [P, 2, N])
        split = sb("split", [P, max(4 * WW, T * (G1 + D) + 4 * N)], F32R)
        zt = sb("zt", [P, 4 * D], F32R)
        x1 = sb("x1", [P, 2, D])
        xt = sb("xt", [P, D])
        z = sb("z", [P, 2, D])
        ztf = sb("ztf", [P, D])
        sm = sb("sm", [P, 16])
        lg = sb("lg", [P, E])
        top = sb("top", [P, 2, 8])
        top_i = sb("top_i", [P, 8], U32)
        hot = sb("hot", [P, TOPK, E])
        hot_pos = sb("hot_pos", [P, TOPK, E])
        mask = sb("mask", [P, 2, E], BF16)
        others = sb("others", [P, P], BF16)
        first_rows = sb("first_rows", [P, E], BF16)
        base0 = sb("base0", [P, E])
        eps = sb("eps", [P, 1])
        warm = sb("warm", [P, 2])
        slot_i = sb("slot_i", [P, 2, TOPK], I32)
        pair = sb("pair", [P, 2, TOPK, 4])
        fill = sb("fill", [P, PAIR_ROWS // P, 4])
        thr = sb("thr", [1, 8])
        tri = sb("tri", [1, E, E])
        iota_s = sb("iota_s", [1, NS])
        tb8 = sb("tb8", [1, 2, E, E])
        cnt = sb("cnt", [1, 3, E])
        ge = sb("ge", [1, 2, NS, E])
        tab_f = sb("tab_f", [1, 4, NS])
        tab = sb("tab", [1, 2, NS], I32)
        turn_slot = sb("turn_slot", [1, TURNS])
        used = sb("used", [1, TURNS])
        last_f = sb("last_f", [1, 1])
        last_turn = sb("last_turn", [1, 1], I32)
        w_raw = sb("w_raw", [P, 2, WW])
        b1_sb = sb("b1_sb", [P, 2, FC])
        b2_sb = sb("b2_sb", [P, 2, D])
        slot_pair = sb("slot_pair", [P, 2, 2, 4])
        kept = sb("kept", [P, 2, 2], I32)
        zg = sb("zg", [P, 2, 2, D])
        h_raw = sb("h_raw", [P, 2, 2 * SLOT])
        h_hi = sb("h_hi", [P, FC, SLOT], F32R)
        h_lo = sb("h_lo", [P, FC, SLOT], F32R)
        ex = sb("ex", [P, 2, 2])
        den = sb("den", [P, 2])
        coef = sb("coef", [P, 2, 2])
        y_b = sb("y_b", [P, 2 * D])
        y_c = sb("y_c", [P, 2, 2, D])

        g_hi = split[:, 0:T * G1].rearrange("p (t c) -> p t c", c=G1)
        g_lo = split[:, T * G1:T * G1 + T * D].rearrange("p (t c) -> p t c", c=D)

        def adj_split(b, part):
            at = T * (G1 + D) + (2 * b + part) * N
            return split[:, at:at + N]

        def w_split(b, part):
            return split[:, (2 * b + part) * WW:(2 * b + part + 1) * WW]

        gw_raw = y_c[:].rearrange("p b j d -> p (b j d)").rearrange("p (c f) -> p c f", c=DC)
        gw_hi = h_hi[:, 0:FC // 2, :].rearrange("p a t -> p (a t)").rearrange("p (c f) -> p c f", c=DC)
        gw_lo = h_hi[:, FC // 2:FC, :].rearrange("p a t -> p (a t)").rearrange("p (c f) -> p c f", c=DC)

        bank = [ctx.enter_context(nc.psum_tensor(f"bank{j}", [P, 512], F32)) for j in range(8)]

        x_in = sems("x_in", 4)
        gw_in, bias_in = sem("gw_in"), sem("bias_in")
        consts = sem("consts")
        fill_ready = sem("fill_ready")
        ones_ready = sem("ones_ready")
        fill_out = sem("fill_out")
        dve_own = sem("dve_own")
        var_all, std_all = sem("var_all"), sem("std_all")
        gw_split = sem("gw_split")
        hn_ready, ht_ps, ht_hi, ht_lo = sem("hn_ready"), sem("ht_ps"), sem("ht_hi"), sem("ht_lo")
        gs_ps, g_hi_ready, g_done = sem("gs_ps"), sem("g_hi_ready"), sem("g_done")
        adj_in = sems("adj_in")
        adj_hi, adj_lo = sem("adj_hi"), sem("adj_lo")
        acc_done, acc_read = sem("acc_done"), sem("acc_read")
        var_ready, std_ready, z_ready = sem("var_ready"), sem("std_ready"), sem("z_ready")
        x1_out, z_out = sems("x1_out"), sems("z_out")
        zt_r_ps, zt_r_sb, logit_ps = sem("zt_r_ps"), sem("zt_r_sb"), sem("logit_ps")
        mask_ready, rank_ps, slot_ready = sem("mask_ready"), sem("rank_ps"), sem("slot_ready")
        route = sem("route")
        hot_used = sem("hot_used")
        pair_ready = sem("pair_ready")
        pair_out = [sems(f"pair_out{b}_") for b in range(2)]
        table_own = sem("table_own")
        table_ready = sem("table_ready")
        w_in, b_in, pair_in = sems("w_in"), sems("b_in"), sems("pair_in")
        w_hi_ready, w_lo_ready = sem("w_hi_ready"), sem("w_lo_ready")
        z_got = [sems(f"z_got{b}_") for b in range(2)]
        zt_ps, zt_hi_ready, zt_lo_ready = sem("zt_ps"), sem("zt_hi_ready"), sem("zt_lo_ready")
        hid_ps, hid_relu, hid_hi, hid_lo = sem("hid_ps"), sem("hid_relu"), sem("hid_hi"), sem("hid_lo")
        ex_ready, coef_step = sem("ex_ready"), sem("coef_step")
        y_ps, y_biased, y_ready = sem("y_ps"), sem("y_biased"), sem("y_ready")
        y_added = sems("y_added")
        idx_kept = sem("idx_kept")
        passed = {e: sem(f"passed_{e}") for e in ("sp", "pool", "dve")}

        NQ = FC // 2
        RELUS = [2 + 6 * (q // 2) + 4 * (q % 2) for q in range(NQ)]
        CHOICE = 4
        LN2 = 8

        def settle(eng, name):
            eng.sem_inc(passed[name], 1)

        def last_of(eng):
            eng.wait_ge(table_ready, 1)
            return eng.value_load(last_turn[0:1, 0:1], min_val=0, max_val=TURNS - 1)

        with nc.Block() as block:

            @block.sync
            def _(sp):
                x_v = x.rearrange("(t p) d -> p t d", p=P)
                for j in range(4):
                    sp.dma_start(x_sb[:, 4 * j:4 * j + 4, :], x_v[:, 4 * j:4 * j + 4, :]).then_inc(x_in[j], 16)
                sp.dma_start(gw_raw[:, :, 0:D], wn_t.rearrange("(c p) f -> p c f", p=P)).then_inc(gw_in, 16)
                sp.dma_start(gw_raw[:, :, D:2 * D], ws_t.rearrange("(c p) f -> p c f", p=P)).then_inc(gw_in, 16)
                sp.dma_start(bias_n[:], b_neigh[None, :].to_broadcast([P, D])).then_inc(bias_in, 16)
                sp.dma_start(bias_s[:], b_self[None, :].to_broadcast([P, D])).then_inc(bias_in, 16)
                sp.dma_start(wg_sb[:], wg.rearrange("(c p) e -> p c e", p=P)).then_inc(bias_in, 16)
                sp.dma_start(bg_sb[:], bg[None, :].to_broadcast([P, E])).then_inc(bias_in, 16)
                for b in range(2):
                    sp.dma_start(adj_raw[:, b, :], adj_t[b]).then_inc(adj_in[b], 16)
                sp.wait_ge(fill_ready, 2)
                sp.dma_start(pairs.rearrange("(p r) w -> p r w", p=P), fill[:]).then_inc(fill_out, 16)
                sp.dma_start(w_raw[:, 0, :], w12[0]).then_inc(w_in[0], 16)
                sp.dma_start(b1_sb[:, 0, :], b1_t[0]).then_inc(b_in[0], 16)
                sp.dma_start(b2_sb[:, 0, :], b2[0:1, :].to_broadcast([P, D])).then_inc(b_in[0], 16)
                for b in range(2):
                    sp.wait_ge(adj_lo, 2 * b + 2)
                    sp.dma_start(adj_raw[:, b, :], adj_t[2 + b]).then_inc(adj_in[b], 16)

                def store(i, b):
                    sp.wait_ge(z_ready, i + 1)
                    sp.dma_start(out[bass.ds(i * P, P), :], x1[:, b, :]).then_inc(x1_out[b], 16)
                    sp.dma_start(z_rows[bass.ds(i * P, P), :], z[:, b, :]).then_inc(z_out[b], 16)

                with sp.Fori(0, T // 2 - 2) as k:
                    for b in range(2):
                        store(2 * k + b, b)
                        sp.wait_ge(adj_lo, 4 * k + 2 * b + 6)
                        sp.dma_start(adj_raw[:, b, :], adj_t[bass.ds(2 * k + b + 4, 1)].rearrange("a p n -> (a p) n")).then_inc(adj_in[b], 16)
                for i in range(T - 4, T):
                    store(i, i % 2)

                def load_pairs(b, at):
                    rows = pairs[bass.ds(at, SLOT), :].rearrange("(j p) w -> p j w", p=P)
                    sp.dma_start(slot_pair[:, b, :, :], rows).then_inc(pair_in[b], 16)

                def first_row(s):
                    return sp.value_load(tab[0:1, 1, bass.ds(s, 1)], min_val=0, max_val=E * N)

                def expert(s):
                    return sp.value_load(tab[0:1, 0, bass.ds(s, 1)], min_val=0, max_val=E - 1)

                def load_weights(b, e):
                    sp.dma_start(w_raw[:, b, :], w12[bass.ds(e, 1)].rearrange("a p n -> (a p) n")).then_inc(w_in[b], 16)

                def hold(s, value):
                    sp.wait_ge(s, value)
                    settle(sp, "sp")

                def ahead(s, b):
                    hold(w_lo_ready, 4 * s + 4)
                    if isinstance(s, int) and s == 0:
                        gathered(1)
                    load_weights(b, expert(s + 2))
                    hold(zt_ps, s + 1)
                    hold(idx_kept, s + 1)
                    hold(ex_ready, s + 1)
                    load_pairs(b, first_row(s + 2))
                    if not isinstance(s, int) or s >= 1:
                        hold(y_biased, s)
                    e = expert(s + 1)
                    sp.dma_start(b1_sb[:, 1 - b, :], b1_t[bass.ds(e, 1)].rearrange("a p n -> (a p) n")).then_inc(b_in[1 - b], 16)
                    sp.dma_start(b2_sb[:, 1 - b, :], b2[bass.ds(e, 1), :].to_broadcast([P, D])).then_inc(b_in[1 - b], 16)

                for b in range(2):
                    for c in range(TOPK):
                        sp.wait_ge(pair_out[b][c], 16 * T // 2)
                load_pairs(0, 0)
                sp.wait_ge(table_ready, 1)
                load_pairs(1, first_row(1))
                last = last_of(sp)

                def gathered(b):
                    for j in range(2):
                        sp.wait_ge(z_got[b][j], 16)
                    settle(sp, "sp")

                gathered(0)
                load_weights(1, expert(1))
                for s in range(2):
                    ahead(s, s)
                with sp.Fori(1, TURNS) as k:
                    with sp.If(k < last + 1):
                        for b in range(2):
                            ahead(2 * k + b, b)
                for j in range(2):
                    hold(y_added[j], 32 * last + 32)
                hold(b_in[0], 32 * last + 64)
                hold(w_in[1], 16 * last + 32)
                for j in range(2):
                    hold(z_got[1][j], 16 * last + 32)
                    sp.wait_ge(x1_out[j], 16 * T // 2)

            @block.gpsimd
            def _(pool):
                pool.memset(ones[:], 1.0).then_inc(ones_ready, 1)
                pool.memset(ident[:], 0.0).then_inc(fill_ready, 1)
                pool.memset(upper[:], 1.0)
                pool.memset(fill[:], 0.0)
                pool.memset(pair[:], 0.0)
                pool.memset(zg[:], 0.0)
                pool.memset(tri[:], 1.0)
                pool.memset(g_hi[:, :, D:D + 1].bitcast(F32), 1.0)
                pool.memset(g_hi[:, :, D + 1:D + 2].bitcast(F32), 0.0)
                pool.iota(thr[:], [[SLOT, 8]], base=0, channel_multiplier=0, allow_small_or_imprecise_dtypes=True)
                pool.iota(iota_s[:], [[1, NS]], base=0, channel_multiplier=0, allow_small_or_imprecise_dtypes=True)
                pool.iota(turn_slot[:], [[2, TURNS]], base=0, channel_multiplier=0, allow_small_or_imprecise_dtypes=True)
                pool.iota(iota_e[:], [[1, E]], base=0, channel_multiplier=0, allow_small_or_imprecise_dtypes=True)
                pool.iota(base0[:], [[N, E]], base=0, channel_multiplier=0, allow_small_or_imprecise_dtypes=True)
                pool.iota(first_rows[:], [[N // P, E]], base=0, channel_multiplier=0, allow_small_or_imprecise_dtypes=True)
                pool.memset(others[:], 1.0)
                pool.memset(eps[:], EPS)
                pool.iota(tokens[:], [[P, T]], base=0, channel_multiplier=1).then_inc(consts, 1)
                pool.wait_ge(consts, 1)
                pool.memset(fill[:, :, 0:1].bitcast(I32), NOWHERE).then_inc(fill_ready, 1)
                pool.affine_select(ident[:], ident[:], [[-1, P]], ALU.not_equal, 1.0, base=0, channel_multiplier=1)
                pool.affine_select(upper[:], upper[:], [[1, P]], ALU.is_gt, 0.0, base=0, channel_multiplier=-1)
                pool.affine_select(others[:], others[:], [[-1, P]], ALU.is_ge, 0.0, base=0, channel_multiplier=1)
                pool.affine_select(tri[:], tri[:], [[1, E], [-1, E]], ALU.is_ge, 0.0, base=0, channel_multiplier=0)
                pool.memset(thr[:, 0:1], -1.0).then_inc(consts, 1)

                pool.wait_ge(fill_out, 16)

                def scatter(i, b, k):
                    pool.wait_ge(mask_ready, i + 1)
                    for c in range(TOPK):
                        pool.wait_ge(pair_out[b][c], 16 * k)
                    t0 = top[:, b, 0:1]
                    pool.tensor_copy(pair[:, b, :, 0:1].bitcast(I32), tokens[:, None, bass.ds(i, 1)].to_broadcast([P, TOPK, 1]))
                    pool.tensor_tensor(pair[:, b, :, 1], top[:, b, 1:2].to_broadcast([P, TOPK]), t0.to_broadcast([P, TOPK]), ALU.subtract)
                    pool.tensor_tensor(pair[:, b, :, 2], top[:, b, 0:TOPK], t0.to_broadcast([P, TOPK]), ALU.subtract).then_inc(pair_ready, 1)
                    pool.wait_ge(pair_ready, i + 1)
                    pool.wait_ge(slot_ready, i + 1)
                    settle(pool, "pool")
                    for c in range(TOPK):
                        pool.indirect_dma_start(pairs, Rows(slot_i[:, b, c:c + 1], 0), pair[:, b, c, :],
                                                None).then_inc(pair_out[b][c], 16)

                with pool.Fori(0, T // 2) as k:
                    for b in range(2):
                        scatter(2 * k + b, b, k)

                for b in range(2):
                    pool.wait_ge(z_out[b], 16 * T // 2)
                    pool.wait_ge(x1_out[b], 16 * T // 2)

                def gather(s, b, k):
                    pool.wait_ge(pair_in[b], 16 * k + 16)
                    if not isinstance(s, int) or s >= 2:
                        pool.wait_ge(zt_ps, s - 1)
                    settle(pool, "pool")
                    for j in range(2):
                        pool.indirect_dma_start(zg[:, b, j, :], None, z_rows, Rows(slot_pair[:, b, j, 0:1].bitcast(I32), 0),
                                                bounds_check=N - 1, oob_is_err=False).then_inc(z_got[b][j], 16)

                def keep(b):
                    pool.tensor_copy(kept[:, b, :, None], slot_pair[:, b, :, 0:1].bitcast(I32)).then_inc(idx_kept, 1)

                def add(s, b):
                    for j in range(2):
                        pool.wait_ge(y_added[j], 16 * s)
                    settle(pool, "pool")
                    keep(1 - b)
                    pool.wait_ge(idx_kept, s + 1)
                    pool.wait_ge(y_ready, 2 * s + 2)
                    settle(pool, "pool")
                    for j in range(2):
                        pool.indirect_dma_start(out, Rows(kept[:, b, j:j + 1], 0), y_c[:, b, j, :], None,
                                                bounds_check=N - 1, oob_is_err=False,
                                                compute_op=ALU.add).then_inc(y_added[j], 16)

                for b in range(2):
                    gather(b, b, 0)
                    if b == 0:
                        keep(b)
                last = last_of(pool)
                with pool.Fori(0, TURNS) as k:
                    with pool.If(k < last + 1):
                        for b in range(2):
                            gather(2 * k + b + 2, b, k + 1)
                            add(2 * k + b, b)

            @block.scalar
            def _(act):
                act.wait_ge(ones_ready, 1)
                act.activation(warm[:, 0:1], ones[:, 0:1], ACT.Sqrt)
                act.wait_ge(gw_in, 32)
                act.activation(gw_hi[:], gw_raw[:], ACT.Copy).then_inc(gw_split, 1)
                act.wait_ge(var_all, 1)
                act.activation(ln[:, 1, :], ln[:, 0, :], ACT.Sqrt).then_inc(std_all, 1)

                def rows_high(i, b):
                    act.wait_ge(ht_ps, i + 1)
                    act.activation(zt[:, 2 * D * b:2 * D * b + D], bank[b][:, 0:D], ACT.Copy).then_inc(ht_hi, 1)

                def features_high(i, b):
                    act.wait_ge(gs_ps, i + 1)
                    act.activation(g_hi[:, bass.ds(i, 1), 0:D], bank[2 + b][:, None, 0:D], ACT.Copy).then_inc(g_hi_ready, 1)

                def high(i, b, half, k):
                    act.wait_ge(adj_in[b], 16 * k + 16)
                    cols = slice(half * HALF, half * HALF + HALF)
                    act.activation(adj_split(b, 0)[:, cols], adj_raw[:, b, cols], ACT.Copy).then_inc(adj_hi, 1)

                rows_high(0, 0)
                with act.Fori(0, T // 2 - 1) as k:
                    for b in range(2):
                        rows_high(2 * k + b + 1, 1 - b)
                        features_high(2 * k + b, b)
                rows_high(T - 1, 1)
                for half, i in enumerate((T - 2, T - 1)):
                    high(0, 0, half, 0)
                    features_high(i, i % 2)

                def root(i):
                    act.wait_ge(var_ready, i + 1)
                    act.activation(sm[:, 4:5], mv[:, 0, 1:2], ACT.Sqrt, bias=eps[:]).then_inc(std_ready, 1)

                def logits_in(i):
                    act.wait_ge(zt_r_ps, i + 1)
                    act.activation(ztf[:], bank[6][:, 0:D], ACT.Copy).then_inc(zt_r_sb, 1)

                for half in range(2):
                    high(1, 1, half, 0)
                for i in range(2):
                    act.wait_ge(acc_done, i + 1)
                    high(i + 2, i, 0, 1)
                    if i > 0:
                        logits_in(i - 1)
                    high(i + 2, i, 1, 1)
                    root(i)
                with act.Fori(1, T // 2 - 1) as k:
                    for b in range(2):
                        i = 2 * k + b
                        act.wait_ge(acc_done, i + 1)
                        high(i + 2, b, 0, k + 1)
                        logits_in(i - 1)
                        high(i + 2, b, 1, k + 1)
                        root(i)
                for i in (T - 2, T - 1):
                    logits_in(i - 1)
                    root(i)
                logits_in(T - 1)
                act.activation(warm[:, 1:2], ones[:, 0:1], ACT.Exp)

                def high_w(b, c, k):
                    act.wait_ge(w_in[b], 16 * k + 16)
                    cols = slice(c * WCH, c * WCH + WCH)
                    act.activation(w_split(b, 0)[:, cols], w_raw[:, b, cols], ACT.Copy).then_inc(w_hi_ready, 1)

                def high_z(s):
                    act.wait_ge(zt_ps, s + 1)
                    act.activation(zt[:, 0:2 * D], bank[6][:], ACT.Copy).then_inc(zt_hi_ready, 1)

                def slot(s, b, k):
                    act.wait_ge(pair_in[b], 16 * k + 16)
                    if not isinstance(s, int) or s >= 1:
                        act.wait_ge(coef_step, 3 * s)
                    act.activation(ex[:], slot_pair[:, b, :, 1:3], ACT.Exp).then_inc(ex_ready, 1)
                    act.wait_ge(b_in[b], 32 * k + 32)
                    if not isinstance(s, int) or s >= 1:
                        act.wait_ge(y_ps, s)
                    if not isinstance(s, int) or s >= 1:
                        high_w(1 - b, 0, k + b)
                    for q in range(NQ):
                        act.wait_ge(hid_ps, NQ * s + q + 1)
                        if not isinstance(s, int) or s > 0 or q >= 2:
                            act.wait_ge(hid_lo, NQ * s + q - 1)
                        for c in range(2):
                            act.activation(h_raw[:, q % 2, c * SLOT:c * SLOT + SLOT], bank[2 + q][:, c * SLOT:c * SLOT + SLOT],
                                           ACT.Relu, bias=b1_sb[:, b, 2 * q + c:2 * q + c + 1]).then_inc(hid_relu, 1)
                            if q % 2:
                                act.activation(h_hi[:, 2 * q + c, :], bank[2 + q][:, c * SLOT:c * SLOT + SLOT],
                                               ACT.Relu, bias=b1_sb[:, b, 2 * q + c:2 * q + c + 1]).then_inc(hid_relu, 1)
                        if q == 0 and (not isinstance(s, int) or s >= 1):
                            results(s - 1, 1 - b)
                    if isinstance(s, int) and s == 0:
                        high_w(1 - b, 0, k + b)
                    high_w(1 - b, 1, k + b)
                    high_z(s + 1)
                    high_w(1 - b, 2, k + b)
                    high_w(1 - b, 3, k + b)

                def results(s, b):
                    act.wait_ge(y_biased, s + 1)
                    act.wait_ge(coef_step, 3 * s + 3)
                    if not isinstance(s, int) or s >= 2:
                        act.wait_ge(y_added[0], 16 * s - 16)
                        act.wait_ge(y_added[1], 16 * s - 16)
                    for j in range(2):
                        act.activation(y_c[:, b, j, :], y_b[:, j * D:j * D + D], ACT.Copy,
                                       scale=coef[:, b, j:j + 1]).then_inc(y_ready, 1)

                act.wait_ge(acc_done, T)
                for c in range(4):
                    high_w(0, c, 0)
                high_z(0)
                for s in range(2):
                    slot(s, s, 0)
                last = last_of(act)
                with act.Fori(1, TURNS) as k:
                    with act.If(k < last + 1):
                        for b in range(2):
                            slot(2 * k + b, b, k)
                results(2 * last + 1, 1)

            @block.vector
            def _(dve):
                own = [0]

                def link(ins):
                    own[0] += 1
                    ins.then_inc(dve_own, 1)
                    dve.wait_ge(dve_own, own[0])

                for j in range(4):
                    dve.wait_ge(x_in[j], 16)
                    for t in range(4 * j, 4 * j + 4):
                        last = dve.bn_stats(stats[:, t, :], x_sb[:, t, :])
                    if j > 0:
                        for t in range(4 * j - 4, 4 * j):
                            dve.bn_aggr(mv[:, t, :], stats[:, t, :])
                    link(last)
                for t in range(T - 4, T):
                    last = dve.bn_aggr(mv[:, t, :], stats[:, t, :])
                link(last)
                dve.tensor_scalar(ln[:, 0, :], mv[:, :, 1], EPS, None, ALU.add).then_inc(var_all, 1)
                dve.wait_ge(std_all, 1)
                link(dve.reciprocal(ln[:, 1, :], ln[:, 1, :]))
                link(dve.tensor_tensor(ln[:, 2, :], ln[:, 0, :], ln[:, 1, :], ALU.mult))
                link(dve.tensor_tensor(ln[:, 2, :], ln[:, 2, :], ln[:, 1, :], ALU.mult))
                link(dve.tensor_scalar(ln[:, 2, :], ln[:, 2, :], -0.5, 1.5, ALU.mult, ALU.add))
                link(dve.tensor_tensor(ln[:, 3, :], ln[:, 1, :], ln[:, 2, :], ALU.mult))

                def normed(i, b):
                    dve.tensor_scalar(hn[:, b, None, :], x_sb[:, bass.ds(i, 1), :], mv[:, bass.ds(i, 1), 0], ln[:, 3, bass.ds(i, 1)],
                                      ALU.subtract, ALU.mult).then_inc(hn_ready, 1)

                normed(0, 0)
                normed(1, 1)
                dve.wait_ge(gw_split, 1)
                dve.tensor_tensor(gw_lo[:], gw_raw[:], gw_hi[:], ALU.subtract).then_inc(gw_split, 1)
                dve.wait_ge(bias_in, 64)
                link(dve.tensor_tensor(bias[:], bias_n[:], bias_s[:], ALU.add))

                def rows_low(i, b, more=True):
                    dve.wait_ge(ht_hi, i + 1)
                    dve.tensor_tensor(zt[:, 2 * D * b + D:2 * D * b + 2 * D], bank[b][:, 0:D], zt[:, 2 * D * b:2 * D * b + D],
                                      ALU.subtract).then_inc(ht_lo, 1)
                    if more:
                        normed(i + 2, b)

                def features(i, b):
                    dve.wait_ge(g_hi_ready, i + 1)
                    dve.tensor_tensor(g_lo[:, bass.ds(i, 1), :], bank[2 + b][:, None, 0:D], g_hi[:, bass.ds(i, 1), 0:D],
                                      ALU.subtract)
                    dve.tensor_tensor(self_sb[:, bass.ds(i, 1), :], bank[2 + b][:, None, D:2 * D], bias[:, None, :],
                                      ALU.add).then_inc(g_done, 1)

                def low(i, b, half, k):
                    dve.wait_ge(adj_hi, 2 * i + half + 1)
                    cols = slice(half * HALF, half * HALF + HALF)
                    dve.tensor_tensor(adj_split(b, 1)[:, cols], adj_raw[:, b, cols], adj_split(b, 0)[:, cols],
                                      ALU.subtract).then_inc(adj_lo, 1)

                rows_low(0, 0)
                with dve.Fori(0, T // 2 - 2) as k:
                    for b in range(2):
                        rows_low(2 * k + b + 1, 1 - b)
                        features(2 * k + b, b)
                for i in range(T - 4, T):
                    if i + 1 < T:
                        rows_low(i + 1, (i + 1) % 2, more=i + 3 < T)
                    features(i, i % 2)
                    if i == T - 2:
                        low(0, 0, 0, 0)

                first = own[0]
                low(0, 0, 1, 0)
                for half in range(2):
                    low(1, 1, half, 0)
                dve.wait_ge(g_done, T)
                dve.wait_ge(consts, 2)

                def pick(i, b, step):
                    if step > 0:
                        dve.wait_ge(route, CHOICE * i + step)
                    if step == 0:
                        dve.wait_ge(logit_ps, i + 1)
                        dve.tensor_tensor(lg[:], bank[7][:, 0:E], bg_sb[:], ALU.add).then_inc(route, 1)
                    if step == 1:
                        if not isinstance(i, int) or i >= 2:
                            dve.wait_ge(pair_ready, i - 1)
                        settle(dve, "dve")
                        dve.max(top[:, b, :], lg[:]).then_inc(route, 1)
                    if step == 2:
                        settle(dve, "dve")
                        dve.max_index(top_i[:], top[:, b, :], lg[:]).then_inc(route, 1)
                    if step == 3:
                        dve.tensor_tensor(hot[:], iota_e[:, None, :].to_broadcast([P, TOPK, E]),
                                          top_i[:, 0:TOPK, None].to_broadcast([P, TOPK, E]), ALU.is_equal).then_inc(route, 1)
                    if step == 4:
                        dve.tensor_tensor(mask[:, b, :], hot[:, 0, :], hot[:, 1, :], ALU.add).then_inc(mask_ready, 1)

                def place(i, b, k, step):
                    if step == 0:
                        dve.wait_ge(rank_ps, i + 1)
                        dve.tensor_tensor(hot_pos[:], hot[:], bank[5][:, None, 0:E].to_broadcast([P, TOPK, E]),
                                          ALU.mult).then_inc(hot_used, 1)
                    if step == 1:
                        if not isinstance(i, int) or i >= 2:
                            for c in range(TOPK):
                                dve.wait_ge(pair_out[b][c], 16 * k)
                        dve.wait_ge(hot_used, i + 1)
                        with nc.allow_low_precision(reason="row numbers, exact in float32 and as integers"):
                            dve.tensor_reduce(slot_i[:, b, :], hot_pos[:], AX.X, ALU.add).then_inc(slot_ready, 1)

                def turn(i, b, k, choose=True, placed=True, lows=True):
                    def after(n, plain=False):
                        dve.wait_ge(dve_own, LN2 * i + first + n)
                        if plain:
                            settle(dve, "dve")

                    dve.wait_ge(acc_done, i + 1)
                    dve.tensor_scalar(sm[:, 0:1], bank[b][:, D:D + 1], EPS, None, ALU.add).then_inc(dve_own, 1)
                    if placed:
                        place(i - 3, 1 - b, k + b - 2, 0)
                    after(1)
                    dve.reciprocal(sm[:, 1:2], sm[:, 0:1]).then_inc(dve_own, 1)
                    if choose:
                        pick(i - 2, b, 0)
                    after(2)
                    dve.scalar_tensor_tensor(out=xt[:, None, :], in0=bank[b][:, None, 0:D], scalar=sm[:, 1:2],
                                             in1=self_sb[:, bass.ds(i, 1), :], op0=ALU.mult, op1=ALU.add).then_inc(acc_read, 1)
                    if placed:
                        place(i - 3, 1 - b, k + b - 2, 1)
                    if choose:
                        pick(i - 2, b, 1)
                    dve.wait_ge(acc_read, i + 1)
                    dve.wait_ge(x1_out[b], 16 * k)
                    dve.wait_ge(z_out[b], 16 * k)
                    dve.scalar_tensor_tensor(out=x1[:, b, None, :], in0=xt[:, None, :], scalar=0.0, in1=x_sb[:, bass.ds(i, 1), :],
                                             op0=ALU.max, op1=ALU.add).then_inc(dve_own, 1)
                    if choose:
                        pick(i - 2, b, 2)
                    if lows:
                        low(i + 2, b, 0, k + 1)
                    after(3)
                    dve.bn_stats(stats[:, 0, :], x1[:, b, :]).then_inc(dve_own, 1)
                    if choose:
                        pick(i - 2, b, 3)
                    after(4, plain=True)
                    dve.bn_aggr(mv[:, 0, :], stats[:, 0, :]).then_inc(var_ready, 1)
                    if choose:
                        pick(i - 2, b, 4)
                    if lows:
                        low(i + 2, b, 1, k + 1)
                    dve.wait_ge(std_ready, i + 1)
                    dve.reciprocal(sm[:, 5:6], sm[:, 4:5]).then_inc(dve_own, 1)
                    after(5)
                    dve.scalar_tensor_tensor(out=sm[:, 6:7], in0=sm[:, 5:6], scalar=-0.5, in1=sm[:, 5:6],
                                             op0=ALU.mult, op1=ALU.mult).then_inc(dve_own, 1)
                    after(6)
                    dve.scalar_tensor_tensor(out=sm[:, 7:8], in0=mv[:, 0, 1:2], scalar=EPS, in1=sm[:, 6:7],
                                             op0=ALU.add, op1=ALU.mult).then_inc(dve_own, 1)
                    after(7)
                    dve.scalar_tensor_tensor(out=sm[:, 8:9], in0=sm[:, 7:8], scalar=1.5, in1=sm[:, 5:6],
                                             op0=ALU.add, op1=ALU.mult).then_inc(dve_own, 1)
                    after(8)
                    dve.tensor_scalar(z[:, b, :], x1[:, b, :], mv[:, 0, 0:1], sm[:, 8:9], ALU.subtract,
                                      ALU.mult).then_inc(z_ready, 1)

                for i in range(4):
                    turn(i, i % 2, i // 2, choose=i >= 2, placed=i >= 3)
                with dve.Fori(2, T // 2 - 1) as k:
                    for b in range(2):
                        turn(2 * k + b, b, k)
                for i in (T - 2, T - 1):
                    turn(i, i % 2, T // 2 - 1, lows=False)
                for i in (T - 3, T - 2, T - 1):
                    if i > T - 3:
                        for step in range(5):
                            pick(i, i % 2, step)
                    for step in range(2):
                        place(i, i % 2, i // 2, step)

                tn = [0]

                def tlink(ins):
                    tn[0] += 1
                    ins.then_inc(table_own, 1)
                    dve.wait_ge(table_own, tn[0])

                r0 = slice(0, 1)
                dve.wait_ge(rank_ps, T + 1)
                tlink(dve.tensor_tensor(cnt[:, 0, :], bank[5][r0, 0:E], base0[r0, :], ALU.subtract))
                tlink(dve.tensor_tensor(tb8[:, 0], cnt[:, 0, :, None].to_broadcast([1, E, E]), thr[:, None, :].to_broadcast([1, E, 8]), ALU.is_gt))
                tlink(dve.tensor_reduce(cnt[:, 1, :], tb8[:, 0], AX.X, ALU.add))
                tlink(dve.tensor_tensor(tb8[:, 1], tri[:], cnt[:, 1, None, :].to_broadcast([1, E, E]), ALU.mult))
                tlink(dve.tensor_reduce(cnt[:, 2, :], tb8[:, 1], AX.X, ALU.add))
                dve.tensor_tensor(used[:], turn_slot[:], cnt[:, 2, E - 1:E].to_broadcast([1, TURNS]), ALU.is_lt)
                tlink(dve.tensor_tensor(ge[:, 0], iota_s[:, :, None].to_broadcast([1, NS, E]), cnt[:, 2, None, :].to_broadcast([1, NS, E]), ALU.is_ge))
                dve.tensor_reduce(last_f[:], used[:], AX.X, ALU.add)
                dve.tensor_reduce(tab_f[:, 0, :], ge[:, 0], AX.X, ALU.add)
                tlink(dve.tensor_tensor(ge[:, 1], ge[:, 0], cnt[:, 1, None, :].to_broadcast([1, NS, E]), ALU.mult))
                tlink(dve.tensor_reduce(tab_f[:, 1, :], ge[:, 1], AX.X, ALU.add))
                tlink(dve.tensor_tensor(tab_f[:, 2, :], iota_s[:], tab_f[:, 1, :], ALU.subtract))
                tlink(dve.tensor_scalar(tab_f[:, 2, :], tab_f[:, 2, :], float(SLOT), None, ALU.mult))
                tlink(dve.scalar_tensor_tensor(out=tab_f[:, 3, :], in0=tab_f[:, 0, :], scalar=float(N), in1=tab_f[:, 2, :],
                                               op0=ALU.mult, op1=ALU.add))
                dve.tensor_scalar(last_turn[:], last_f[:], -1.0, None, ALU.add)
                dve.tensor_scalar(tab[:, 0, :], tab_f[:, 0, :], float(E - 1), None, ALU.min)
                dve.tensor_scalar(tab[:, 1, :], tab_f[:, 3, :], float(E * N), None, ALU.min).then_inc(table_ready, 1)

                def low_w(b, c, s):
                    dve.wait_ge(w_hi_ready, 4 * s + c + 1)
                    cols = slice(c * WCH, c * WCH + WCH)
                    dve.tensor_tensor(w_split(b, 1)[:, cols], w_raw[:, b, cols], w_split(b, 0)[:, cols],
                                      ALU.subtract).then_inc(w_lo_ready, 1)

                def low_z(s):
                    dve.wait_ge(zt_hi_ready, s + 1)
                    dve.tensor_tensor(zt[:, 2 * D:4 * D], bank[6][:], zt[:, 0:2 * D], ALU.subtract).then_inc(zt_lo_ready, 1)

                def slot(s, b):
                    dve.wait_ge(ex_ready, s + 1)
                    if not isinstance(s, int) or s >= 2:
                        dve.wait_ge(y_ready, 2 * s - 2)
                    dve.tensor_scalar(den[:], ex[:, :, 0], 1.0, None, ALU.add).then_inc(coef_step, 1)
                    dve.wait_ge(coef_step, 3 * s + 1)
                    dve.reciprocal(den[:], den[:]).then_inc(coef_step, 1)
                    dve.wait_ge(coef_step, 3 * s + 2)
                    dve.tensor_tensor(coef[:, b, :], den[:], ex[:, :, 1], ALU.mult).then_inc(coef_step, 1)
                    if not isinstance(s, int) or s >= 1:
                        low_w(1 - b, 0, s + 1)
                    for q in range(NQ):
                        dve.wait_ge(hid_relu, RELUS[-1] * s + RELUS[q])
                        raw = h_raw[:, q % 2, :]
                        hi = h_hi[:, 2 * q:2 * q + 2, :].rearrange("p a t -> p (a t)")
                        if q % 2 == 0:
                            dve.tensor_copy(hi, raw).then_inc(hid_hi, 1)
                            dve.wait_ge(hid_hi, NQ // 2 * s + q // 2 + 1)
                        dve.tensor_tensor(h_lo[:, 2 * q:2 * q + 2, :].rearrange("p a t -> p (a t)"), raw, hi,
                                          ALU.subtract).then_inc(hid_lo, 1)
                    if isinstance(s, int) and s == 0:
                        low_w(1 - b, 0, s + 1)
                    low_w(1 - b, 1, s + 1)
                    low_z(s + 1)
                    low_w(1 - b, 2, s + 1)
                    low_w(1 - b, 3, s + 1)
                    dve.wait_ge(y_ps, s + 1)
                    if not isinstance(s, int) or s >= 1:
                        dve.wait_ge(y_ready, 2 * s)
                    dve.tensor_tensor(y_b[:].rearrange("p (j d) -> p j d", j=2), bank[b][:].rearrange("p (j d) -> p j d", j=2),
                                      b2_sb[:, b, None, :].to_broadcast([P, 2, D]), ALU.add).then_inc(y_biased, 1)

                for c in range(4):
                    low_w(0, c, 0)
                low_z(0)
                for s in range(2):
                    slot(s, s)
                last = last_of(dve)
                with dve.Fori(1, TURNS) as k:
                    with dve.If(k < last + 1):
                        for b in range(2):
                            slot(2 * k + b, b)

            @block.tensor
            def _(pe):
                pe.wait_ge(consts, 2)

                def rows_t(i, b):
                    pe.wait_ge(hn_ready, i + 1)
                    if not isinstance(i, int) or i >= 2:
                        pe.wait_ge(ht_lo, i - 1)
                    for c in range(DC):
                        last = pe.transpose(bank[b][:, c * P:c * P + P], hn[:, b, c * P:c * P + P], ident[:])
                    last.then_inc(ht_ps, 1)

                def products(out_ap, terms):
                    for n, (o, w, m) in enumerate(terms):
                        last = pe.matmul(o, w, m, start=(n == 0), stop=(n == len(terms) - 1), skip_group_check=True)
                    return last

                def features(i, b):
                    pe.wait_ge(ht_lo, i + 1)
                    if not isinstance(i, int) or i >= 2:
                        pe.wait_ge(g_done, i - 1)
                    hi, lo = zt[:, 2 * D * b:2 * D * b + D], zt[:, 2 * D * b + D:2 * D * b + 2 * D]
                    terms = []
                    for c in range(DC):
                        cc = slice(c * P, c * P + P)
                        terms += [(bank[2 + b][:], hi[:, cc], gw_hi[:, c, :]), (bank[2 + b][:], hi[:, cc], gw_lo[:, c, :]),
                                  (bank[2 + b][:], lo[:, cc], gw_hi[:, c, :])]
                    products(None, terms).then_inc(gs_ps, 1)

                rows_t(0, 0)
                rows_t(1, 1)
                pe.wait_ge(gw_split, 2)
                for i in range(2):
                    features(i, i)
                    rows_t(i + 2, i)
                with pe.Fori(1, T // 2 - 1) as k:
                    for b in range(2):
                        features(2 * k + b, b)
                        rows_t(2 * k + b + 2, b)
                for i in (T - 2, T - 1):
                    features(i, i % 2)

                def aggregate(b, j0, j1):
                    hi, lo = adj_split(b, 0), adj_split(b, 1)
                    for j in range(j0, j1):
                        jj = slice(j * P, j * P + P)
                        pe.matmul(bank[b][:, 0:G1], hi[:, jj], g_hi[:, j, :], start=(j == 0), stop=False, skip_group_check=True)
                        pe.matmul(bank[b][:, 0:D], hi[:, jj], g_lo[:, j, :], start=False, stop=False, skip_group_check=True)
                        last = pe.matmul(bank[b][:, 0:G1], lo[:, jj], g_hi[:, j, :], start=False, stop=(j == T - 1),
                                         skip_group_check=True)
                    return last

                def transpose_z(i, b):
                    pe.wait_ge(z_ready, i + 1)
                    if not isinstance(i, int) or i >= 1:
                        pe.wait_ge(zt_r_sb, i)
                    for c in range(DC):
                        last = pe.transpose(bank[6][:, c * P:c * P + P], z[:, b, c * P:c * P + P], ident[:])
                    last.then_inc(zt_r_ps, 1)

                def logits(i):
                    pe.wait_ge(zt_r_sb, i + 1)
                    if not isinstance(i, int) or i >= 1:
                        pe.wait_ge(route, CHOICE * i - CHOICE + 1)
                    for c in range(DC):
                        last = pe.matmul(bank[7][:, 0:E], ztf[:, c * P:c * P + P], wg_sb[:, c, :], start=(c == 0), stop=(c == DC - 1))
                    last.then_inc(logit_ps, 1)

                def ranks(i, b):
                    if isinstance(i, int) and i == 0:
                        pe.matmul(bank[5][:, 0:E], ones[:], first_rows[:], start=True, stop=True, skip_group_check=True)
                    else:
                        pe.wait_ge(hot_used, i)
                        pe.matmul(bank[5][:, 0:E], others[:], mask[:, 1 - b, :], start=False, stop=True, skip_group_check=True)
                    pe.wait_ge(mask_ready, i + 1)
                    pe.matmul(bank[5][:, 0:E], upper[:], mask[:, b, :], start=False, stop=True,
                              skip_group_check=True).then_inc(rank_ps, 1)

                def tile(i, b, back=3):
                    pe.wait_ge(adj_lo, 2 * i + 1)
                    if back >= 2:
                        pe.wait_ge(acc_read, i - 1)
                    aggregate(b, 0, T // 4)
                    if back >= 2:
                        transpose_z(i - 2, b)
                    aggregate(b, T // 4, T // 2)
                    pe.wait_ge(adj_lo, 2 * i + 2)
                    if back >= 2:
                        logits(i - 2)
                    aggregate(b, T // 2, T - 2)
                    if back >= 3:
                        ranks(i - 3, 1 - b)
                    aggregate(b, T - 2, T).then_inc(acc_done, 1)

                pe.wait_ge(g_done, T)
                for i in range(4):
                    tile(i, i % 2, back=i)
                with pe.Fori(2, T // 2) as k:
                    for b in range(2):
                        tile(2 * k + b, b)
                transpose_z(T - 2, 0)
                ranks(T - 3, 1)
                logits(T - 2)
                transpose_z(T - 1, 1)
                logits(T - 1)
                ranks(T - 2, 0)
                ranks(T - 1, 1)
                pe.wait_ge(hot_used, T)
                pe.matmul(bank[5][:, 0:E], others[:], mask[:, 1, :], start=False, stop=True,
                          skip_group_check=True).then_inc(rank_ps, 1)

                def transpose_slot(s, b, k):
                    for j in range(2):
                        pe.wait_ge(z_got[b][j], 16 * k + 16)
                    if not isinstance(s, int) or s >= 1:
                        pe.wait_ge(zt_lo_ready, s)
                    for j in range(2):
                        for c in range(DC):
                            last = pe.transpose(bank[6][:, c * SLOT + j * P:c * SLOT + j * P + P], zg[:, b, j, c * P:c * P + P], ident[:])
                    last.then_inc(zt_ps, 1)

                def slot(s, b, k):
                    w_hi, w_lo = w_split(b, 0), w_split(b, 1)
                    z_hi, z_lo = zt[:, 0:2 * D], zt[:, 2 * D:4 * D]
                    pe.wait_ge(zt_lo_ready, s + 1)
                    pe.wait_ge(w_lo_ready, 4 * s + 2)
                    for q in range(NQ):
                        if not isinstance(s, int) or s >= 1:
                            pe.wait_ge(hid_relu, RELUS[-1] * (s - 1) + RELUS[q])
                        for c in range(2):
                            o = bank[2 + q][:, c * SLOT:c * SLOT + SLOT]
                            terms = []
                            for d in range(DC):
                                f = slice(d * F + (2 * q + c) * P, d * F + (2 * q + c) * P + P)
                                t = slice(d * SLOT, d * SLOT + SLOT)
                                terms += [(o, w_hi[:, f], z_hi[:, t]), (o, w_hi[:, f], z_lo[:, t]), (o, w_lo[:, f], z_hi[:, t])]
                            last = products(o, terms)
                        last.then_inc(hid_ps, 1)
                    transpose_slot(s + 1, 1 - b, k + b)
                    pe.wait_ge(w_lo_ready, 4 * s + 4)
                    if not isinstance(s, int) or s >= 2:
                        pe.wait_ge(y_biased, s - 1)
                    for j in range(2):
                        o = bank[b][:, j * D:j * D + D]
                        t = slice(j * P, j * P + P)
                        for c in range(FC):
                            if j == 0 and c % 2 == 0:
                                pe.wait_ge(hid_lo, NQ * s + c // 2 + 1)
                            d = slice(DC * F + c * D, DC * F + c * D + D)
                            pe.matmul(o, h_hi[:, c, t], w_hi[:, d], start=(c == 0), stop=False, skip_group_check=True)
                            pe.matmul(o, h_hi[:, c, t], w_lo[:, d], start=False, stop=False, skip_group_check=True)
                            last = pe.matmul(o, h_lo[:, c, t], w_hi[:, d], start=False, stop=(c == FC - 1), skip_group_check=True)
                    last.then_inc(y_ps, 1)

                transpose_slot(0, 0, 0)
                for s in range(2):
                    slot(s, s, 0)
                last = last_of(pe)
                with pe.Fori(1, TURNS) as k:
                    with pe.If(k < last + 1):
                        for b in range(2):
                            slot(2 * k + b, b, k)


def kernel(x, adj, L0_gnn_W_neigh, L0_gnn_b_neigh, L0_gnn_W_self, L0_gnn_b_self, L0_ffn_Wg, L0_ffn_bg,
           L0_ffn_W1, L0_ffn_b1, L0_ffn_W2, L0_ffn_b2):
    import numpy as np
    import concourse.bacc as bacc
    from concourse.bass_utils import run_bass_kernel_spmd

    x, adj, w1, b1, w2, b2 = (np.asarray(a) for a in (x, adj, L0_ffn_W1, L0_ffn_b1, L0_ffn_W2, L0_ffn_b2))
    n, (e, d, f) = x.shape[0], w1.shape
    t, dc, fc = n // P, d // P, f // P
    arrays = {
        "x": x,
        "adj_t": adj.reshape(t, P, t, P).transpose(0, 3, 2, 1).reshape(t, P, n),
        "wn_t": np.asarray(L0_gnn_W_neigh).T,
        "ws_t": np.asarray(L0_gnn_W_self).T,
        "b_neigh": np.asarray(L0_gnn_b_neigh),
        "b_self": np.asarray(L0_gnn_b_self),
        "wg": np.asarray(L0_ffn_Wg),
        "bg": np.asarray(L0_ffn_bg),
        "w12": np.concatenate([w1.reshape(e, dc, P, f).transpose(0, 2, 1, 3).reshape(e, P, dc * f),
                               w2.reshape(e, fc, P, d).transpose(0, 2, 1, 3).reshape(e, P, fc * d)], axis=2),
        "b1_t": b1.reshape(e, fc, P).transpose(0, 2, 1),
        "b2": b2,
    }
    nc = bacc.Bacc("TRN2", target_bir_lowering=False, num_devices=1)
    args = {}
    for name, a in arrays.items():
        arrays[name] = a = np.ascontiguousarray(a)
        args[name] = nc.dram_tensor(name, a.shape, mybir.dt.from_np(a.dtype), kind="ExternalInput").ap()
    out = nc.dram_tensor("out", x.shape, F32, kind="ExternalOutput").ap()
    gnn_moe_kernel(nc, out=out, **args)
    return run_bass_kernel_spmd(nc, [arrays], core_ids=[0]).results[0]["out"]
```
